# Optimizing a Trainium2 kernel written in Bass

```python
import numpy as np
import jax
import jax.numpy as jnp

def _softmax(x, axis=-1):
    return jax.nn.softmax(x, axis=axis)

def _gelu(x):
    return jax.nn.gelu(x, approximate=True)

def _silu(x):
    return jax.nn.silu(x)

def _sigmoid(x):
    return jax.nn.sigmoid(x)

def _layernorm(x, axis=-1, eps=1e-05):
    m = jnp.mean(x, axis=axis, keepdims=True)
    v = jnp.var(x, axis=axis, keepdims=True)
    return (x - m) / jnp.sqrt(v + eps)

def _scatter_add(tgt, idx, src, axis=0):
    return tgt.at[idx].add(src)

def _segment_sum(src, seg, n):
    return jax.ops.segment_sum(src, seg, n)
kernel_name = 'mk_dlrm_tower_d1_rec_r8_417f01'

def setup_inputs(seed: int=0):
    np.random.seed(seed)
    _w = jnp.asarray

    def _rec_inputs():
        import jax
        import jax.numpy as jnp
        _tk = jax.random.key(seed)
        ids = jnp.stack([jax.random.randint(jax.random.fold_in(_tk, 200 + f), (2048,), 0, v, jnp.int32) for f, v in enumerate([12500, 1250, 125000, 1250, 1000, 1000, 12500, 1250, 12500, 1250, 1000, 12500, 1000, 12500, 12500, 12500, 1000, 1250, 12500, 1000, 1000, 1250, 1250, 1250, 1000, 1000])], axis=1)
        tbl_0 = 0.05 * jax.random.normal(jax.random.fold_in(_tk, 500 + 0), (12500, 128), jnp.float32)
        tbl_1 = 0.05 * jax.random.normal(jax.random.fold_in(_tk, 500 + 1), (1250, 128), jnp.float32)
        tbl_2 = 0.05 * jax.random.normal(jax.random.fold_in(_tk, 500 + 2), (125000, 128), jnp.float32)
        tbl_3 = 0.05 * jax.random.normal(jax.random.fold_in(_tk, 500 + 3), (1250, 128), jnp.float32)
        tbl_4 = 0.05 * jax.random.normal(jax.random.fold_in(_tk, 500 + 4), (1000, 128), jnp.float32)
        tbl_5 = 0.05 * jax.random.normal(jax.random.fold_in(_tk, 500 + 5), (1000, 128), jnp.float32)
        tbl_6 = 0.05 * jax.random.normal(jax.random.fold_in(_tk, 500 + 6), (12500, 128), jnp.float32)
        tbl_7 = 0.05 * jax.random.normal(jax.random.fold_in(_tk, 500 + 7), (1250, 128), jnp.float32)
        tbl_8 = 0.05 * jax.random.normal(jax.random.fold_in(_tk, 500 + 8), (12500, 128), jnp.float32)
        tbl_9 = 0.05 * jax.random.normal(jax.random.fold_in(_tk, 500 + 9), (1250, 128), jnp.float32)
        tbl_10 = 0.05 * jax.random.normal(jax.random.fold_in(_tk, 500 + 10), (1000, 128), jnp.float32)
        tbl_11 = 0.05 * jax.random.normal(jax.random.fold_in(_tk, 500 + 11), (12500, 128), jnp.float32)
        tbl_12 = 0.05 * jax.random.normal(jax.random.fold_in(_tk, 500 + 12), (1000, 128), jnp.float32)
        tbl_13 = 0.05 * jax.random.normal(jax.random.fold_in(_tk, 500 + 13), (12500, 128), jnp.float32)
        tbl_14 = 0.05 * jax.random.normal(jax.random.fold_in(_tk, 500 + 14), (12500, 128), jnp.float32)
        tbl_15 = 0.05 * jax.random.normal(jax.random.fold_in(_tk, 500 + 15), (12500, 128), jnp.float32)
        tbl_16 = 0.05 * jax.random.normal(jax.random.fold_in(_tk, 500 + 16), (1000, 128), jnp.float32)
        tbl_17 = 0.05 * jax.random.normal(jax.random.fold_in(_tk, 500 + 17), (1250, 128), jnp.float32)
        tbl_18 = 0.05 * jax.random.normal(jax.random.fold_in(_tk, 500 + 18), (12500, 128), jnp.float32)
        tbl_19 = 0.05 * jax.random.normal(jax.random.fold_in(_tk, 500 + 19), (1000, 128), jnp.float32)
        tbl_20 = 0.05 * jax.random.normal(jax.random.fold_in(_tk, 500 + 20), (1000, 128), jnp.float32)
        tbl_21 = 0.05 * jax.random.normal(jax.random.fold_in(_tk, 500 + 21), (1250, 128), jnp.float32)
        tbl_22 = 0.05 * jax.random.normal(jax.random.fold_in(_tk, 500 + 22), (1250, 128), jnp.float32)
        tbl_23 = 0.05 * jax.random.normal(jax.random.fold_in(_tk, 500 + 23), (1250, 128), jnp.float32)
        tbl_24 = 0.05 * jax.random.normal(jax.random.fold_in(_tk, 500 + 24), (1000, 128), jnp.float32)
        tbl_25 = 0.05 * jax.random.normal(jax.random.fold_in(_tk, 500 + 25), (1000, 128), jnp.float32)
        _rk = jax.random.fold_in(_tk, 7)
        r_dense_features = -0.000520686 + 1.00062 * jax.random.normal(jax.random.fold_in(_rk, 101), (2048, 128), jnp.float32)
        W_top1 = 0.0405887 * jax.random.normal(jax.random.fold_in(_tk, 801), (607, 512), jnp.float32)
        W_top2 = 0.0441942 * jax.random.normal(jax.random.fold_in(_tk, 802), (512, 256), jnp.float32)
        W_top3 = 0.0625 * jax.random.normal(jax.random.fold_in(_tk, 803), (256, 1), jnp.float32)
        b_top1 = jnp.zeros((512,), jnp.float32)
        b_top2 = jnp.zeros((256,), jnp.float32)
        return (r_dense_features, ids, tbl_0, tbl_1, tbl_2, tbl_3, tbl_4, tbl_5, tbl_6, tbl_7, tbl_8, tbl_9, tbl_10, tbl_11, tbl_12, tbl_13, tbl_14, tbl_15, tbl_16, tbl_17, tbl_18, tbl_19, tbl_20, tbl_21, tbl_22, tbl_23, tbl_24, tbl_25, W_top1, b_top1, W_top2, b_top2, W_top3)
    r_dense_features, ids, tbl_0, tbl_1, tbl_2, tbl_3, tbl_4, tbl_5, tbl_6, tbl_7, tbl_8, tbl_9, tbl_10, tbl_11, tbl_12, tbl_13, tbl_14, tbl_15, tbl_16, tbl_17, tbl_18, tbl_19, tbl_20, tbl_21, tbl_22, tbl_23, tbl_24, tbl_25, W_top1, b_top1, W_top2, b_top2, W_top3 = _rec_inputs()

    def _L0_rec_setup():
        import jax, jax.numpy as jnp
        import numpy as np
        NUM_SPARSE = 26
        EMBED_DIM = 128
        BATCH = 2048
        key = jax.random.key(seed)
        k1, k2 = jax.random.split(key)
        dense_features = jax.random.normal(k1, (BATCH, EMBED_DIM), dtype=jnp.float32)
        sparse_features = jax.random.normal(k2, (BATCH, NUM_SPARSE, EMBED_DIM), dtype=jnp.float32)
        return {'dense_features': dense_features, 'sparse_features': sparse_features}
    _L0_rec_all = _L0_rec_setup()
    _L0_rec_in = {k: v for k, v in _L0_rec_all.items() if k in ()}
    del _L0_rec_all
    return {'r_dense_features': r_dense_features, 'ids': ids, 'tbl_0': tbl_0, 'tbl_1': tbl_1, 'tbl_2': tbl_2, 'tbl_3': tbl_3, 'tbl_4': tbl_4, 'tbl_5': tbl_5, 'tbl_6': tbl_6, 'tbl_7': tbl_7, 'tbl_8': tbl_8, 'tbl_9': tbl_9, 'tbl_10': tbl_10, 'tbl_11': tbl_11, 'tbl_12': tbl_12, 'tbl_13': tbl_13, 'tbl_14': tbl_14, 'tbl_15': tbl_15, 'tbl_16': tbl_16, 'tbl_17': tbl_17, 'tbl_18': tbl_18, 'tbl_19': tbl_19, 'tbl_20': tbl_20, 'tbl_21': tbl_21, 'tbl_22': tbl_22, 'tbl_23': tbl_23, 'tbl_24': tbl_24, 'tbl_25': tbl_25, 'W_top1': W_top1, 'b_top1': b_top1, 'W_top2': W_top2, 'b_top2': b_top2, 'W_top3': W_top3}

def reference(r_dense_features, ids, tbl_0, tbl_1, tbl_2, tbl_3, tbl_4, tbl_5, tbl_6, tbl_7, tbl_8, tbl_9, tbl_10, tbl_11, tbl_12, tbl_13, tbl_14, tbl_15, tbl_16, tbl_17, tbl_18, tbl_19, tbl_20, tbl_21, tbl_22, tbl_23, tbl_24, tbl_25, W_top1, b_top1, W_top2, b_top2, W_top3):
    import jax
    import jax.numpy as jnp

    def _L0_rec_ref(dense_features, sparse_features):
        import jax, jax.numpy as jnp
        import numpy as np
        NUM_SPARSE = 26
        EMBED_DIM = 128
        BATCH = 2048
        F = NUM_SPARSE + 1
        combined = jnp.concatenate([dense_features[:, None, :], sparse_features], axis=1)
        interactions = jnp.einsum('bfd,bgd->bfg', combined, combined)
        iu, ju = jnp.triu_indices(F, k=1)
        interactions_flat = interactions[:, iu, ju]
        return jnp.concatenate([dense_features, interactions_flat], axis=1)
    e = jnp.stack([tbl_0[ids[:, 0]], tbl_1[ids[:, 1]], tbl_2[ids[:, 2]], tbl_3[ids[:, 3]], tbl_4[ids[:, 4]], tbl_5[ids[:, 5]], tbl_6[ids[:, 6]], tbl_7[ids[:, 7]], tbl_8[ids[:, 8]], tbl_9[ids[:, 9]], tbl_10[ids[:, 10]], tbl_11[ids[:, 11]], tbl_12[ids[:, 12]], tbl_13[ids[:, 13]], tbl_14[ids[:, 14]], tbl_15[ids[:, 15]], tbl_16[ids[:, 16]], tbl_17[ids[:, 17]], tbl_18[ids[:, 18]], tbl_19[ids[:, 19]], tbl_20[ids[:, 20]], tbl_21[ids[:, 21]], tbl_22[ids[:, 22]], tbl_23[ids[:, 23]], tbl_24[ids[:, 24]], tbl_25[ids[:, 25]]], axis=1)
    z = _L0_rec_ref(r_dense_features, e)
    z = z.reshape(z.shape[0], -1)
    h = jnp.concatenate([z, r_dense_features], axis=1)
    h = jnp.maximum(h @ W_top1 + b_top1, 0.0)
    h = jnp.maximum(h @ W_top2 + b_top2, 0.0)
    y = h @ W_top3
    return y

_drawn_inputs = setup_inputs


def setup_inputs(seed=0):
    import zlib

    import numpy as np

    out = dict(_drawn_inputs(seed))
    spreads = {'b_top1': (0.0, 0.1), 'b_top2': (0.0, 0.1)}
    factors = {}
    for name, (base, spread) in spreads.items():
        noise = np.random.default_rng([zlib.crc32(name.encode()), seed]).standard_normal(out[name].shape)
        drawn = base * np.exp(spread * noise) if base else spread * noise
        out[name] = jnp.asarray(drawn.astype(out[name].dtype))
    for name, factor in factors.items():
        out[name] = (out[name] * factor).astype(out[name].dtype)
    return out
```

```python
import concourse.bass as bass
from concourse import mybir
from contextlib import ExitStack

F32 = mybir.dt.float32
F32R = mybir.dt.float32r
I32 = mybir.dt.int32
ALU = mybir.AluOpType
ACT = mybir.ActivationFunctionType

P = 128
BATCH = 2048
N_SPARSE = 26
FEATS = N_SPARSE + 1
DIM = 128
PAIRS = FEATS * (FEATS - 1) // 2
HID1, HID2 = 512, 256

SUB = 128
BLOCK = 2 * SUB
BLOCKS = BATCH // BLOCK
COLS = 4
QUADS = BLOCK // COLS
HALF_QUADS = SUB // COLS // 2

ONEHOT_BANKS = [(5, 6), (11, 13), (17, 20), (21, 25), (26,)]
ONEHOT_FEATS = [f for bank in ONEHOT_BANKS for f in bank]
N_OH = len(ONEHOT_FEATS)
OH_ROWS = 1000
KT = 8
KROWS = OH_ROWS // KT
OH_ALL = N_OH * KT
OH_RING = 12
OH_CHUNK = 4
ROW_BANKS = [(0, 1, 2, 3), (4, 8, 12, 16), (7, 10, 15, 18), (9, 14, 19, 24), (22, 23)]
ROW_FEATS = [f for bank in ROW_BANKS for f in bank]
XB = len(ROW_BANKS)
OB = len(ONEHOT_BANKS)

Z_ONE = PAIRS
Z_COLS = PAIRS + 1
Z_TILES = [(0, 128), (128, 128), (256, Z_COLS - 256)]
PAIR_BASE = [sum(FEATS - 1 - i for i in range(c)) for c in range(FEATS)]
XT_COLS = SUB * FEATS + 32 - (FEATS - 1)
N_PAIRED = (FEATS - 1) // 2


def features(view, feats):
    f0 = feats[0]
    steps = {b - a for a, b in zip(feats, feats[1:])}
    if len(feats) == 1:
        return view[:, f0:f0 + 1, :]
    if len(steps) == 1:
        step = steps.pop()
        return view[:, f0:feats[-1] + 1:step, :]
    inner, outer = feats[1] - f0, feats[2] - f0
    both = view[:, f0:f0 + 2 * outer, :].rearrange("p (a e) b -> p a e b", e=outer)
    return both[:, :, 0:inner + 1:inner, :]


def as_pairs(tile, feats):
    steps = {b - a for a, b in zip(feats, feats[1:])}
    if len(steps) > 1:
        return tile.rearrange("p (a e b) -> p a e b", a=2, e=2)
    return tile.rearrange("p (f b) -> p f b", f=len(feats))


def build(nc, dense, ids, ids_onehot, tables, W1, b1, W2, b2, W3, y):
    ctx = ExitStack()
    with ctx:
        def sb(name, shape, dt=F32):
            return ctx.enter_context(nc.sbuf_tensor(name, shape, dt))

        def bank(name):
            return ctx.enter_context(nc.psum_tensor(name, [P, 512], F32))

        def sem(name):
            return ctx.enter_context(nc.semaphore(name))

        ident = sb("ident", [P, P])
        row_id = sb("row_id", [P, KT])
        tab_high = sb("tab_high", [P, N_OH, KT, DIM], F32R)
        tab_low = sb("tab_low", [P, N_OH, KT, DIM], F32R)
        stage = sb("stage", [P, 2, KT * DIM])
        ids_b = sb("ids_b", [P, N_OH, BLOCK], I32)
        onehot = sb("onehot", [P, OH_RING, BLOCK], F32R)
        idx = sb("idx", [P, 2, N_SPARSE], I32)
        rows = sb("rows", [P, 2, len(ROW_FEATS), DIM])
        XT = sb("XT", [P, 2, XT_COLS])
        xd_high = sb("xd_high", [P, COLS, QUADS], F32R)
        xd_low = sb("xd_low", [P, COLS, QUADS], F32R)
        G = sb("G", [P, FEATS - 1, QUADS])
        Z = sb("Z", [QUADS, COLS, Z_COLS])
        zt_high = sb("zt_high", [P, 3, BLOCK], F32R)
        zt_low = sb("zt_low", [P, 3, BLOCK], F32R)
        w1_high = sb("w1_high", [P, 4, HID1], F32R)
        w1_low = sb("w1_low", [P, 4, HID1], F32R)
        w2_high = sb("w2_high", [P, 4, HID2], F32R)
        w2_low = sb("w2_low", [P, 4, HID2], F32R)
        w3 = sb("w3", [P, 2])
        b2_sb = sb("b2_sb", [P, 2])
        h1_high = sb("h1_high", [P, 4, BLOCK], F32R)
        h1_low = sb("h1_low", [P, 4, BLOCK], F32R)
        h2 = sb("h2", [P, 2, BLOCK])
        assert 2 * KT * DIM >= BATCH
        y_sb = stage[0:1, :, :].rearrange("p i n -> p (i n)")

        bank_x = [bank(f"bank_x{i}") for i in range(2)]
        bank_oh = [bank(f"bank_oh{i}") for i in range(2)]
        bank_c = [bank(f"bank_c{i}") for i in range(2)]
        bank_m = [bank(f"bank_m{i}") for i in range(2)]
        bank_t = [bank_c[0], bank_c[1], bank_m[0], bank_m[1]]
        T_ON_ACT = (1, 2)
        T_PAIRS = [range(4 * k, min(4 * k + 4, N_PAIRED)) for k in range(4)]

        consts_ready = sem("consts_ready")
        pads_ready = sem("pads_ready")
        small_ready = sem("small_ready")
        stage_in = [sem(f"stage_in{i}") for i in range(2)]
        dense_w_sum = sem("dense_w_sum")
        split_high = sem("split_high")
        split_low = sem("split_low")
        idx_ready = [sem(f"idx_ready{j}") for j in range(2)]
        dense_ready = [sem(f"dense_ready{j}") for j in range(2)]
        rows_ready = [[sem(f"rows_ready{j}_{g}") for g in range(XB)] for j in range(2)]
        gather_go = sem("gather_go")
        ids_ready = sem("ids_ready")
        onehot_made = sem("onehot_made")
        onehot_used = sem("onehot_used")
        oh_evac = sem("oh_evac")
        x_done = sem("x_done")
        x_evac = sem("x_evac")
        xd_high_ready = sem("xd_high_ready")
        xd_low_ready = sem("xd_low_ready")
        gram_done = sem("gram_done")
        g_evac = sem("g_evac")
        t_done = sem("t_done")
        t_evac_dve = sem("t_evac_dve")
        t_evac_act = sem("t_evac_act")
        zt_done = sem("zt_done")
        z_go = sem("z_go")
        z_high_ready = sem("z_high_ready")
        z_low_ready = sem("z_low_ready")
        l1_done = sem("l1_done")
        h1_high_ready = sem("h1_high_ready")
        h1_low_ready = sem("h1_low_ready")
        l2_done = sem("l2_done")
        h2_ready = sem("h2_ready")
        l3_done = sem("l3_done")
        y_ready = sem("y_ready")
        y_out = sem("y_out")

        W_DENSE, W_PAIRS_A, W_PAIRS_B, W_2 = range(N_OH, N_OH + 4)
        ITEMS = N_OH + 4

        def staged(i):
            s = stage[:, i % 2, :]
            if i < N_OH:
                v = s.rearrange("p (t d) -> p t d", t=KT)
                return v[0:KROWS], tab_high[0:KROWS, i], tab_low[0:KROWS, i]
            if i == W_DENSE:
                return s[:, 0:HID1], w1_high[:, 0, :], w1_low[:, 0, :]
            if i == W_PAIRS_A:
                v = s.rearrange("p (t n) -> p t n", t=2)
                return v, w1_high[:, 1:3, :], w1_low[:, 1:3, :]
            if i == W_PAIRS_B:
                k = Z_TILES[2][1]
                return s[0:k, 0:HID1], w1_high[0:k, 3, :], w1_low[0:k, 3, :]
            return s.rearrange("p (t n) -> p t n", t=4), w2_high[:, :, :], w2_low[:, :, :]

        def stage_arrived(i):
            return 32 * (i // 2 + 1)

        xt_feat = [XT[:, j, 0:SUB * FEATS].rearrange("p (b f) -> p f b", f=FEATS) for j in range(2)]

        block = ctx.enter_context(nc.Block())

        @block.sync
        def _(sp):
            def load_idx(j, n):
                at = n * BLOCK + j * SUB
                sp.dma_start(idx[:, j, :], ids[bass.ds(at, SUB), :]).then_inc(idx_ready[j], 16)

            def load_dense(j, n):
                at = n * BLOCK + j * SUB
                sp.dma_start(rows[:, j, 0, :], dense[bass.ds(at, SUB), :]).then_inc(dense_ready[j], 16)

            def load_item(i):
                s = stage[:, i % 2, :]
                done = stage_in[i % 2]
                if i < N_OH:
                    v = tables[ONEHOT_FEATS[i] - 1].rearrange("(p t) d -> p (t d)", t=KT)
                    sp.dma_start(s[0:112, :], v[0:112, :]).then_inc(done, 16)
                    sp.dma_start(s[112:KROWS, :], v[112:KROWS, :]).then_inc(done, 16)
                elif i == W_DENSE:
                    sp.dma_start(s[:, 0:HID1], W1[0:DIM, :]).then_inc(done, 16)
                    sp.dma_start(s[:, HID1:2 * HID1], W1[DIM + PAIRS:, :]).then_inc(done, 16)
                elif i == W_PAIRS_A:
                    for t in range(2):
                        sp.dma_start(s[:, t * HID1:(t + 1) * HID1],
                                     W1[DIM + t * P:DIM + (t + 1) * P, :]).then_inc(done, 16)
                elif i == W_PAIRS_B:
                    k = Z_TILES[2][1] - 1
                    sp.dma_start(s[0:k, 0:HID1], W1[DIM + 2 * P:DIM + PAIRS, :]).then_inc(done, 16)
                    sp.dma_start(s[k:k + 1, 0:HID1], b1).then_inc(done, 16)
                else:
                    v = W2.rearrange("(t p) n -> p t n", p=P)
                    sv = s.rearrange("p (t n) -> p t n", t=4)
                    for t in range(0, 4, 2):
                        sp.dma_start(sv[:, t:t + 2, :], v[:, t:t + 2, :]).then_inc(done, 16)

            load_idx(0, 0)
            load_idx(1, 0)
            sp.dma_start(ids_b[:, :, :], ids_onehot[:, 0:BLOCK].partition_broadcast(P)).then_inc(ids_ready, 16)
            load_item(0)
            load_item(1)
            load_dense(0, 0)
            load_dense(1, 0)
            sp.dma_start(b2_sb[:, :], b2).then_inc(small_ready, 16)
            sp.dma_start(w3[:, :], W3).then_inc(small_ready, 16)
            for i in range(2, ITEMS):
                sp.wait_ge(split_low, i - 1)
                load_item(i)
            with sp.Fori(0, BLOCKS - 1) as n:
                for j in range(2):
                    for g in range(XB):
                        gathers = len(ROW_BANKS[g]) - (g == 0)
                        sp.wait_ge(rows_ready[j][g], n * (16 * gathers) + 16 * gathers)
                    load_idx(j, n + 1)
                    sp.wait_ge(x_done, n * (2 * XB) + (XB * j + 1))
                    load_dense(j, n + 1)

        @block.gpsimd
        def _(pool):
            nc.gpsimd.memset(ident[:, :], 0.0).then_inc(consts_ready, 1)
            pool.wait_ge(consts_ready, 1)
            nc.gpsimd.affine_select(out=ident[:, :], in_=ident[:, :], compare_op=ALU.not_equal, fill=1.0,
                                    base=0, pattern=[[-1, P]], channel_multiplier=1).then_inc(consts_ready, 1)
            nc.gpsimd.iota(row_id[:, :], pattern=[[1, KT]], base=0, channel_multiplier=KT,
                           allow_small_or_imprecise_dtypes=True).then_inc(consts_ready, 1)

            def gather(n, first):
                for j in range(2):
                    pool.wait_ge(idx_ready[j], n * 16 + 16)
                    at = 0
                    for g, feats in enumerate(ROW_BANKS):
                        if not first:
                            pool.wait_ge(x_done, n * (2 * XB) + (XB * j + g + 1 - 2 * XB))
                            pool.sem_inc(gather_go, 1)
                        for f in feats:
                            if f:
                                nc.gpsimd.indirect_dma_start(
                                    out=rows[:, j, at, :], out_offset=None, in_=tables[f - 1],
                                    in_offset=bass.IndirectOffsetOnAxis(ap=idx[:, j, f - 1:f], axis=0),
                                ).then_inc(rows_ready[j][g], 16)
                            at += 1

            gather(0, True)
            with pool.Fori(1, BLOCKS) as n:
                gather(n, False)

        @block.tensor
        def _(pe):
            def transpose_rows(n, j):
                at = 0
                for g, feats in enumerate(ROW_BANKS):
                    gathers = len(feats) - (g == 0)
                    if g == 0:
                        pe.wait_ge(dense_ready[j], n * 16 + 16)
                    pe.wait_ge(rows_ready[j][g], n * (16 * gathers) + 16 * gathers)
                    if g >= 2:
                        pe.wait_ge(x_evac, n * (2 * XB) + (XB * j + g - 1))
                    for i in range(len(feats)):
                        last = nc.tensor.transpose(bank_x[(XB * j + g) % 2][:, i * SUB:(i + 1) * SUB],
                                                   rows[:, j, at, :], ident[:, :])
                        at += 1
                    last.then_inc(x_done, 1)

            def interactions(n, j):
                pe.wait_ge(pads_ready, 1)
                pe.wait_ge(x_evac, n * (2 * XB) + XB * (j + 1))
                if j == 0:
                    pe.wait_ge(oh_evac, n * OB + OB)
                for h in range(2):
                    if j == 1:
                        pe.wait_ge(g_evac, n * 4 + (h + 1))
                    for q in range(HALF_QUADS):
                        for s in range(COLS):
                            at = (s * 2 * HALF_QUADS + h * HALF_QUADS + q) * FEATS
                            last = nc.tensor.matmul(
                                bank_c[h][32 * s:32 * s + 32, q * (FEATS - 1):(q + 1) * (FEATS - 1)],
                                XT[:, j, at + 1:at + 33], XT[:, j, at:at + FEATS - 1],
                                start=True, stop=True, tile_position=(0, 32 * s))
                    last.then_inc(gram_done, 1)

            def lookup_bank(n, g, split_waits=False):
                feats = ONEHOT_BANKS[g]
                if g >= 2:
                    pe.wait_ge(oh_evac, n * OB + (g - 1))
                for i, f in enumerate(feats):
                    t = ONEHOT_FEATS.index(f)
                    if split_waits:
                        pe.wait_ge(split_low, t + 1)
                    out = bank_oh[g % 2][:, i * BLOCK:(i + 1) * BLOCK]
                    for k in range(KT):
                        at = t * KT + k
                        if at % OH_CHUNK == 0:
                            pe.wait_ge(onehot_made, n * OH_ALL + (at + OH_CHUNK))
                        moving = onehot[0:KROWS, at % OH_RING, :]
                        nc.tensor.matmul(out, tab_high[0:KROWS, t, k, :], moving, start=(k == 0), stop=False)
                        last = nc.tensor.matmul(out, tab_low[0:KROWS, t, k, :], moving,
                                                start=False, stop=(k == KT - 1))
                        if at % OH_CHUNK == OH_CHUNK - 1:
                            last.then_inc(onehot_used, 1)

            def transpose_g(n):
                pe.wait_ge(g_evac, n * 4 + 4)
                for k, pairs in enumerate(T_PAIRS):
                    for i, c2 in enumerate(pairs):
                        both = G[:, 2 * c2:2 * c2 + 2, :].rearrange("p c q -> p (c q)")
                        last = nc.tensor.transpose(bank_t[k][:, i * P:(i + 1) * P], both, ident[:, :])
                    last.then_inc(t_done, 1)

            def transpose_z(n):
                pe.wait_ge(t_evac_dve, n * 2 + 2)
                pe.wait_ge(t_evac_act, n * 2 + 2)
                pe.wait_ge(pads_ready, 1)
                pe.sem_inc(z_go, 1)
                for t, (c0, size) in enumerate(Z_TILES):
                    for s in range(COLS):
                        at = (t % 2) * BLOCK + s * QUADS
                        last = nc.tensor.transpose(bank_c[t // 2][0:size, at:at + QUADS],
                                                   Z[:, s, c0:c0 + size], ident[0:QUADS, 0:QUADS])
                    if t:
                        last.then_inc(zt_done, 1)

            def split_products(out, terms):
                for i, (w_h, w_l, a_h, a_l) in enumerate(terms):
                    nc.tensor.matmul(out, w_h, a_h, start=(i == 0), stop=False)
                    nc.tensor.matmul(out, w_h, a_l, start=False, stop=False)
                    last = nc.tensor.matmul(out, w_l, a_h, start=False, stop=(i == len(terms) - 1))
                return last

            def layer1(n):
                pe.wait_ge(split_low, ITEMS)
                pe.wait_ge(xd_high_ready, n * 2 + 2)
                pe.wait_ge(xd_low_ready, n * 2 + 2)
                pe.wait_ge(z_high_ready, n * 2 + 2)
                pe.wait_ge(z_low_ready, n * 2 + 2)
                xh = xd_high[:, :, :].rearrange("p s q -> p (s q)")
                xl = xd_low[:, :, :].rearrange("p s q -> p (s q)")
                for m in range(HID1 // P):
                    mm = slice(m * P, (m + 1) * P)
                    terms = [(w1_high[:, 0, mm], w1_low[:, 0, mm], xh, xl)]
                    for t, (_, size) in enumerate(Z_TILES):
                        terms.append((w1_high[0:size, t + 1, mm], w1_low[0:size, t + 1, mm],
                                      zt_high[0:size, t, :], zt_low[0:size, t, :]))
                    last = split_products(bank_m[m // 2][:, (m % 2) * BLOCK:(m % 2 + 1) * BLOCK], terms)
                    if m % 2:
                        last.then_inc(l1_done, 1)

            def layer2(n):
                pe.wait_ge(h1_high_ready, n * 2 + 2)
                pe.wait_ge(h1_low_ready, n * 2 + 2)
                for m in range(HID2 // P):
                    mm = slice(m * P, (m + 1) * P)
                    terms = [(w2_high[:, t, mm], w2_low[:, t, mm], h1_high[:, t, :], h1_low[:, t, :])
                             for t in range(HID1 // P)]
                    last = split_products(bank_c[0][:, m * BLOCK:(m + 1) * BLOCK], terms)
                last.then_inc(l2_done, 1)

            def layer3(n):
                pe.wait_ge(h2_ready, n * 2 + 2)
                for m in range(HID2 // P):
                    last = nc.tensor.matmul(bank_c[1][0:1, 0:BLOCK], w3[:, m:m + 1], h2[:, m, :],
                                            start=(m == 0), stop=(m == HID2 // P - 1))
                last.then_inc(l3_done, 1)

            def steps(n, last_block):
                transpose_rows(n, 0)
                interactions(n, 0)
                transpose_rows(n, 1)
                interactions(n, 1)
                tail = [transpose_g, transpose_z, layer1, layer2, layer3]
                for g in range(OB):
                    if not last_block:
                        lookup_bank(n + 1, g)
                    tail[g](n)

            pe.wait_ge(consts_ready, 3)
            for g in range(OB):
                lookup_bank(0, g, split_waits=True)
            pe.wait_ge(small_ready, 32)
            with pe.Fori(0, BLOCKS - 1) as n:
                steps(n, False)
            steps(BLOCKS - 1, True)

        def z_copies(k):
            for i, c2 in enumerate(T_PAIRS[k]):
                for half in range(2):
                    c = 2 * c2 + half
                    src = bank_t[k][half * QUADS:(half + 1) * QUADS, i * P:(i + 1) * P]
                    src = src.rearrange("p (s f) -> p s f", s=COLS)[:, :, c:FEATS - 1]
                    yield Z[:, :, PAIR_BASE[c]:PAIR_BASE[c] + FEATS - 1 - c], src

        @block.scalar
        def _(act):
            def round_item(i):
                src, high, _ = staged(i)
                act.wait_ge(stage_in[i % 2], stage_arrived(i))
                if i == W_DENSE:
                    act.wait_ge(dense_w_sum, 1)
                nc.scalar.copy(high, src).then_inc(split_high, 1)

            def lookups_to_xt(n, g):
                feats = ONEHOT_BANKS[g]
                chunks = sum(len(b) for b in ONEHOT_BANKS[:g + 1]) * KT // OH_CHUNK
                act.wait_ge(onehot_used, n * (OH_ALL // OH_CHUNK) + chunks)
                src = bank_oh[g % 2][:, 0:len(feats) * BLOCK].rearrange("p (f b) -> p f b", f=len(feats))
                for j in range(2):
                    last = nc.scalar.copy(features(xt_feat[j], feats), src[:, :, j * SUB:(j + 1) * SUB])
                last.then_inc(oh_evac, 1)

            def rows_to_xt(n, j):
                for g, feats in enumerate(ROW_BANKS):
                    act.wait_ge(x_done, n * (2 * XB) + (XB * j + g + 1))
                    src = bank_x[(XB * j + g) % 2][:, 0:len(feats) * SUB]
                    nc.scalar.copy(features(xt_feat[j], feats), as_pairs(src, feats)).then_inc(x_evac, 1)
                act.wait_ge(x_evac, n * (2 * XB) + (XB * j + 1))
                src = xt_feat[j][:, 0, :].rearrange("p (s q) -> p s q", s=COLS)
                nc.scalar.copy(xd_high[:, :, 32 * j:32 * j + 32], src).then_inc(xd_high_ready, 1)

            def t_to_z(n):
                for i, k in enumerate(T_ON_ACT):
                    act.wait_ge(t_done, n * 4 + (k + 1))
                    for dst, src in z_copies(k):
                        last = nc.scalar.copy(dst, src)
                    last.then_inc(t_evac_act, 1)

            def round_z(n):
                act.wait_ge(zt_done, n * 2 + 1)
                nc.scalar.copy(zt_high[:, 0:2, :],
                               bank_c[0][:, :].rearrange("p (t b) -> p t b", t=2)).then_inc(z_high_ready, 1)
                act.wait_ge(zt_done, n * 2 + 2)
                k = Z_TILES[2][1]
                nc.scalar.copy(zt_high[0:k, 2, :], bank_c[1][0:k, 0:BLOCK]).then_inc(z_high_ready, 1)

            def round_h1(n):
                for i in range(2):
                    act.wait_ge(l1_done, n * 2 + (i + 1))
                    nc.scalar.activation(h1_high[:, 2 * i:2 * i + 2, :].rearrange("p t b -> p (t b)"),
                                         bank_m[i][:, :], ACT.Relu).then_inc(h1_high_ready, 1)

            def relu_h2(n):
                act.wait_ge(l2_done, n + 1)
                for m in range(2):
                    nc.scalar.activation(h2[:, m, :], bank_c[0][:, m * BLOCK:(m + 1) * BLOCK], ACT.Relu,
                                         bias=b2_sb[:, m:m + 1]).then_inc(h2_ready, 1)

            def copy_y(n):
                act.wait_ge(l3_done, n + 1)
                src = bank_c[1][0:1, 0:BLOCK].rearrange("p (s j q) -> p j s q", s=COLS, j=2)
                dst = y_sb[:, bass.ds(n * BLOCK, BLOCK)].rearrange("p (j s q) -> p j s q", s=COLS, j=2)
                nc.scalar.copy(dst, src).then_inc(y_ready, 1)

            def steps(n, last_block):
                if not last_block:
                    act.wait_ge(onehot_made, n * OH_ALL + OH_ALL)
                    act.dma_start(ids_b[:, :, :],
                                  ids_onehot[:, bass.ds(n * BLOCK + BLOCK, BLOCK)].partition_broadcast(P)
                                  ).then_inc(ids_ready, 16)
                rows_to_xt(n, 0)
                rows_to_xt(n, 1)
                tail = [t_to_z, round_z, round_h1, relu_h2, copy_y]
                for g in range(OB):
                    if not last_block:
                        if g == 0:
                            act.wait_ge(gram_done, n * 4 + 4)
                        lookups_to_xt(n + 1, g)
                    tail[g](n)

            for i in range(4):
                round_item(i)
            for g in range(OB):
                lookups_to_xt(0, g)
                for i in range(4 + 2 * g, min(6 + 2 * g, N_OH)):
                    round_item(i)
            for i in range(N_OH, ITEMS):
                round_item(i)
            act.wait_ge(small_ready, 32)
            with act.Fori(0, BLOCKS - 1) as n:
                steps(n, False)
            steps(BLOCKS - 1, True)
            act.wait_ge(y_ready, BLOCKS)
            act.dma_start(y, y_sb[:, :]).then_inc(y_out, 16)
            act.wait_ge(y_out, 16)

        @block.vector
        def _(dve):
            def remainder(i):
                src, high, low = staged(i)
                if i == W_DENSE:
                    dve.wait_ge(stage_in[i % 2], stage_arrived(i))
                    s = stage[:, i % 2, :]
                    nc.vector.tensor_tensor(s[:, 0:HID1], s[:, 0:HID1], s[:, HID1:2 * HID1],
                                            ALU.add).then_inc(dense_w_sum, 1)
                dve.wait_ge(split_high, i + 1)
                nc.vector.tensor_tensor(low, src, high.bitcast(F32), ALU.subtract).then_inc(split_low, 1)

            def make_onehots(n, lo, hi, first=False):
                for at in range(lo, hi):
                    if at % OH_CHUNK == 0 and not (first and at < OH_RING):
                        dve.wait_ge(onehot_used, n * (OH_ALL // OH_CHUNK)
                                    + (at + OH_CHUNK - OH_RING) // OH_CHUNK)
                    t, k = divmod(at, KT)
                    nc.vector.tensor_scalar(onehot[0:KROWS, at % OH_RING, :], ids_b[0:KROWS, t, :],
                                            row_id[0:KROWS, k:k + 1], None,
                                            ALU.is_equal).then_inc(onehot_made, 1)

            def g_from_psum(n, j):
                for h in range(2):
                    dve.wait_ge(gram_done, n * 4 + (2 * j + h + 1))
                    q0 = (2 * j + h) * HALF_QUADS
                    dst = G[:, :, q0:q0 + HALF_QUADS].rearrange("p c q -> p q c")
                    src = bank_c[h][:, 0:HALF_QUADS * (FEATS - 1)].rearrange("p (q c) -> p q c", q=HALF_QUADS)
                    nc.vector.tensor_copy(dst, src).then_inc(g_evac, 1)

            def dense_low(n, j):
                dve.wait_ge(xd_high_ready, n * 2 + (j + 1))
                src = xt_feat[j][:, 0, :].rearrange("p (s q) -> p s q", s=COLS)
                at = slice(32 * j, 32 * j + 32)
                nc.vector.tensor_tensor(xd_low[:, :, at], src, xd_high[:, :, at].bitcast(F32),
                                        ALU.subtract).then_inc(xd_low_ready, 1)

            def t_to_z(n, k):
                dve.wait_ge(t_done, n * 4 + (k + 1))
                for dst, src in z_copies(k):
                    last = nc.vector.tensor_copy(dst, src)
                last.then_inc(t_evac_dve, 1)

            def z_low(n):
                dve.wait_ge(z_high_ready, n * 2 + 1)
                nc.vector.tensor_tensor(zt_low[:, 0:2, :], bank_c[0][:, :].rearrange("p (t b) -> p t b", t=2),
                                        zt_high[:, 0:2, :].bitcast(F32), ALU.subtract).then_inc(z_low_ready, 1)
                dve.wait_ge(z_high_ready, n * 2 + 2)
                k = Z_TILES[2][1]
                nc.vector.tensor_tensor(zt_low[0:k, 2, :], bank_c[1][0:k, 0:BLOCK],
                                        zt_high[0:k, 2, :].bitcast(F32), ALU.subtract).then_inc(z_low_ready, 1)

            def h1_remainder(n):
                for i in range(2):
                    dve.wait_ge(h1_high_ready, n * 2 + (i + 1))
                    high = h1_high[:, 2 * i:2 * i + 2, :].rearrange("p t b -> p (t b)")
                    low = h1_low[:, 2 * i:2 * i + 2, :].rearrange("p t b -> p (t b)")
                    nc.vector.scalar_tensor_tensor(out=low, in0=bank_m[i][:, :], scalar=0.0,
                                                   in1=high.bitcast(F32), op0=ALU.max,
                                                   op1=ALU.subtract).then_inc(h1_low_ready, 1)

            def steps(n, last_block):
                def onehots(lo, hi):
                    if not last_block:
                        if lo == 0:
                            dve.wait_ge(ids_ready, n * 16 + 32)
                        make_onehots(n + 1, lo, hi)

                onehots(0, 12)
                dense_low(n, 0)
                g_from_psum(n, 0)
                dense_low(n, 1)
                g_from_psum(n, 1)
                onehots(12, 24)
                t_to_z(n, 0)
                t_to_z(n, 3)
                onehots(24, 44)
                z_low(n)
                onehots(44, 60)
                h1_remainder(n)
                onehots(60, OH_ALL)

            for j in range(2):
                nc.vector.memset(XT[:, j, SUB * FEATS:], 0.0)
            nc.vector.memset(Z[:, :, Z_ONE:Z_ONE + 1], 1.0).then_inc(pads_ready, 1)
            dve.wait_ge(consts_ready, 3)
            dve.wait_ge(ids_ready, 16)
            make_onehots(0, 0, KT, first=True)
            for i in range(N_OH):
                remainder(i)
                if i:
                    make_onehots(0, i * KT, (i + 1) * KT, first=True)
            for i in range(N_OH, ITEMS):
                remainder(i)
            with dve.Fori(0, BLOCKS - 1) as n:
                steps(n, False)
            steps(BLOCKS - 1, True)


def kernel(**inputs):
    import numpy as np
    import concourse.bacc as bacc
    from concourse.bass_utils import run_bass_kernel_spmd

    nc = bacc.Bacc("TRN2", target_bir_lowering=False, num_devices=1)
    ids = np.asarray(inputs["ids"])
    arrays = {
        "dense": inputs["r_dense_features"],
        "ids": ids,
        "ids_onehot": ids.T[[f - 1 for f in ONEHOT_FEATS]],
        "W1": inputs["W_top1"],
        "b1": np.asarray(inputs["b_top1"]).reshape(1, HID1),
        "W2": inputs["W_top2"],
        "b2": np.asarray(inputs["b_top2"]).reshape(HID2 // P, P).T,
        "W3": np.asarray(inputs["W_top3"]).reshape(HID2 // P, P).T,
    }
    for t in range(N_SPARSE):
        arrays[f"tbl_{t}"] = inputs[f"tbl_{t}"]
    arrays = {k: np.ascontiguousarray(v) for k, v in arrays.items()}
    ap = {k: nc.dram_tensor(f"{k}_dram", v.shape, mybir.dt.from_np(v.dtype), kind="ExternalInput").ap()
          for k, v in arrays.items()}
    y = nc.dram_tensor("y_dram", (1, BATCH), F32, kind="ExternalOutput").ap()
    build(nc, ap["dense"], ap["ids"], ap["ids_onehot"], [ap[f"tbl_{t}"] for t in range(N_SPARSE)],
          ap["W1"], ap["b1"], ap["W2"], ap["b2"], ap["W3"], y)
    r = run_bass_kernel_spmd(nc, [{f"{k}_dram": v for k, v in arrays.items()}], core_ids=[0])
    return r.results[0]["y_dram"].reshape(BATCH, 1)
```

```python
import concourse.bass as bass
from concourse import mybir
from contextlib import ExitStack

F32 = mybir.dt.float32
F32R = mybir.dt.float32r
I32 = mybir.dt.int32
ALU = mybir.AluOpType
ACT = mybir.ActivationFunctionType

P = 128
BATCH = 2048
N_SPARSE = 26
FEATS = N_SPARSE + 1
DIM = 128
PAIRS = FEATS * (FEATS - 1) // 2
HID1, HID2 = 512, 256

SUB = 128
BLOCK = 2 * SUB
BLOCKS = BATCH // BLOCK
COLS = 4
QUADS = BLOCK // COLS
HALF_QUADS = SUB // COLS // 2

ONEHOT_BANKS = [(5, 6), (11, 13), (17, 20), (25, 26)]
ONEHOT_FEATS = [f for bank in ONEHOT_BANKS for f in bank]
N_OH = len(ONEHOT_FEATS)
OH_ROWS = 1000
KT = 8
KROWS = OH_ROWS // KT
OH_ALL = N_OH * KT
OH_RING = 16
OH_CHUNK = 4
OH_PARTS = [(0, 4), (4, N_OH)]
OH_BEFORE = (2, 4, 6, 7, N_OH)
ROW_BANKS = [(0, 1, 2, 3), (4, 8, 12, 16), (7, 10, 15, 18), (9, 14, 19, 24), (21, 22, 23)]
ROWS_ON_DVE = (1, 3)
ROW_FEATS = [f for bank in ROW_BANKS for f in bank]
XB = len(ROW_BANKS)
OB = len(ONEHOT_BANKS)

Z_ONE = PAIRS
Z_COLS = PAIRS + 1
Z_TILES = [(0, 128), (128, 128), (256, Z_COLS - 256)]
PAIR_BASE = [sum(FEATS - 1 - i for i in range(c)) for c in range(FEATS)]
N_PAIRED = (FEATS - 1) // 2


def features(view, feats):
    f0 = feats[0]
    steps = {b - a for a, b in zip(feats, feats[1:])}
    if len(feats) == 1:
        return view[:, f0:f0 + 1, :]
    if len(steps) == 1:
        step = steps.pop()
        return view[:, f0:feats[-1] + 1:step, :]
    inner, outer = feats[1] - f0, feats[2] - f0
    both = view[:, f0:f0 + 2 * outer, :].rearrange("p (a e) b -> p a e b", e=outer)
    return both[:, :, 0:inner + 1:inner, :]


def as_pairs(tile, feats):
    steps = {b - a for a, b in zip(feats, feats[1:])}
    if len(steps) > 1:
        return tile.rearrange("p (a e b) -> p a e b", a=2, e=2)
    return tile.rearrange("p (f b) -> p f b", f=len(feats))


def build(nc, dense, ids, ids_onehot, tables, W1, b1, W2, b2, W3, y):
    ctx = ExitStack()
    with ctx:
        def sb(name, shape, dt=F32):
            return ctx.enter_context(nc.sbuf_tensor(name, shape, dt))

        def bank(name):
            return ctx.enter_context(nc.psum_tensor(name, [P, 512], F32))

        def sem(name):
            return ctx.enter_context(nc.semaphore(name))

        ident = sb("ident", [P, P])
        row_id = sb("row_id", [P, KT])
        tab_high = sb("tab_high", [P, N_OH, KT, DIM], F32R)
        tab_low = sb("tab_low", [P, N_OH, KT, DIM], F32R)
        stage = sb("stage", [P, 2, KT * DIM])
        ids_b = sb("ids_b", [P, N_OH, BLOCK], I32)
        onehot = sb("onehot", [P, OH_RING, BLOCK], F32R)
        idx = sb("idx", [P, 2, N_SPARSE], I32)
        rows = sb("rows", [P, 2, len(ROW_FEATS), DIM])
        XT = sb("XT", [P, 2, SUB * FEATS])
        xd_high = sb("xd_high", [P, COLS, QUADS], F32R)
        xd_low = sb("xd_low", [P, COLS, QUADS], F32R)
        G = sb("G", [P, FEATS - 1, QUADS])
        Z = sb("Z", [QUADS, COLS, Z_COLS])
        zt_high = sb("zt_high", [P, 3, BLOCK], F32R)
        zt_low = sb("zt_low", [P, 3, BLOCK], F32R)
        w1_high = sb("w1_high", [P, 4, HID1], F32R)
        w1_low = sb("w1_low", [P, 4, HID1], F32R)
        w2_high = sb("w2_high", [P, 4, HID2], F32R)
        w2_low = sb("w2_low", [P, 4, HID2], F32R)
        w3 = sb("w3", [P, 2])
        b2_sb = sb("b2_sb", [P, 2])
        h1_high = sb("h1_high", [P, 4, BLOCK], F32R)
        h1_low = sb("h1_low", [P, 4, BLOCK], F32R)
        h2 = sb("h2", [P, 2, BLOCK])
        assert 2 * KT * DIM >= BATCH
        y_sb = stage[0:1, :, :].rearrange("p i n -> p (i n)")

        bank_x = [bank(f"bank_x{i}") for i in range(2)]
        bank_oh = [bank(f"bank_oh{i}") for i in range(2)]
        bank_c = [bank(f"bank_c{i}") for i in range(2)]
        bank_m = [bank(f"bank_m{i}") for i in range(2)]
        bank_t = [bank_c[0], bank_c[1], bank_m[0], bank_m[1]]
        bank_r = [bank_x[0], bank_x[1], bank_m[0], bank_m[1]]
        T_PAIRS = [range(4 * k, min(4 * k + 4, N_PAIRED)) for k in range(4)]

        consts_ready = sem("consts_ready")
        pads_ready = sem("pads_ready")
        small_ready = sem("small_ready")
        stage_in = [sem(f"stage_in{i}") for i in range(2)]
        dense_w_sum = sem("dense_w_sum")
        split_high = sem("split_high")
        split_low = sem("split_low")
        idx_ready = [sem(f"idx_ready{j}") for j in range(2)]
        dense_ready = [sem(f"dense_ready{j}") for j in range(2)]
        rows_ready = [[sem(f"rows_ready{j}_{g}") for g in range(XB)] for j in range(2)]
        gather_go = sem("gather_go")
        ids_ready = [sem(f"ids_ready{i}") for i in range(2)]
        onehot_made = sem("onehot_made")
        onehot_used = sem("onehot_used")
        oh_evac = sem("oh_evac")
        x_done = sem("x_done")
        x_evac_act = sem("x_evac_act")
        x_evac_dve = sem("x_evac_dve")
        X_ACT, X_DVE = XB - len(ROWS_ON_DVE), len(ROWS_ON_DVE)
        xd_high_ready = sem("xd_high_ready")
        xd_low_ready = sem("xd_low_ready")
        gram_done = sem("gram_done")
        g_evac = sem("g_evac")
        t_done = sem("t_done")
        t_evac = sem("t_evac")
        zt_done = sem("zt_done")
        z_go = sem("z_go")
        z_high_ready = sem("z_high_ready")
        z_low_ready = sem("z_low_ready")
        l1_done = sem("l1_done")
        h1_high_ready = sem("h1_high_ready")
        h1_low_ready = sem("h1_low_ready")
        l2_done = sem("l2_done")
        h2_ready = sem("h2_ready")
        l3_done = sem("l3_done")
        y_ready = sem("y_ready")
        y_out = sem("y_out")

        W_DENSE, W_PAIRS_A, W_PAIRS_B, W_2 = "dense", "pairs_a", "pairs_b", "w2"
        ITEMS = list(range(N_OH))
        for place, w in ((4, W_DENSE), (6, W_PAIRS_A), (8, W_PAIRS_B), (10, W_2)):
            ITEMS.insert(place, w)

        def staged(i):
            s, what = stage[:, i % 2, :], ITEMS[i]
            if what == W_DENSE:
                return s[:, 0:HID1], w1_high[:, 0, :], w1_low[:, 0, :]
            if what == W_PAIRS_A:
                v = s.rearrange("p (t n) -> p t n", t=2)
                return v, w1_high[:, 1:3, :], w1_low[:, 1:3, :]
            if what == W_PAIRS_B:
                k = Z_TILES[2][1]
                return s[0:k, 0:HID1], w1_high[0:k, 3, :], w1_low[0:k, 3, :]
            if what == W_2:
                return s.rearrange("p (t n) -> p t n", t=4), w2_high[:, :, :], w2_low[:, :, :]
            v = s.rearrange("p (t d) -> p t d", t=KT)
            return v[0:KROWS], tab_high[0:KROWS, what], tab_low[0:KROWS, what]

        def stage_arrived(i):
            return 32 * (i // 2 + 1)

        xt_feat = [XT[:, j, :].rearrange("p (b f) -> p f b", f=FEATS) for j in range(2)]

        block = ctx.enter_context(nc.Block())

        @block.sync
        def _(sp):
            def load_idx(j, n):
                at = n * BLOCK + j * SUB
                sp.dma_start(idx[:, j, :], ids[bass.ds(at, SUB), :]).then_inc(idx_ready[j], 16)

            def load_dense(j, n):
                at = n * BLOCK + j * SUB
                sp.dma_start(rows[:, j, 0, :], dense[bass.ds(at, SUB), :]).then_inc(dense_ready[j], 16)

            def load_item(i):
                s = stage[:, i % 2, :]
                done = stage_in[i % 2]
                if ITEMS[i] == W_DENSE:
                    sp.dma_start(s[:, 0:HID1], W1[0:DIM, :]).then_inc(done, 16)
                    sp.dma_start(s[:, HID1:2 * HID1], W1[DIM + PAIRS:, :]).then_inc(done, 16)
                elif ITEMS[i] == W_PAIRS_A:
                    for t in range(2):
                        sp.dma_start(s[:, t * HID1:(t + 1) * HID1],
                                     W1[DIM + t * P:DIM + (t + 1) * P, :]).then_inc(done, 16)
                elif ITEMS[i] == W_PAIRS_B:
                    k = Z_TILES[2][1] - 1
                    sp.dma_start(s[0:k, 0:HID1], W1[DIM + 2 * P:DIM + PAIRS, :]).then_inc(done, 16)
                    sp.dma_start(s[k:k + 1, 0:HID1], b1).then_inc(done, 16)
                elif ITEMS[i] == W_2:
                    v = W2.rearrange("(t p) n -> p t n", p=P)
                    sv = s.rearrange("p (t n) -> p t n", t=4)
                    for t in range(0, 4, 2):
                        sp.dma_start(sv[:, t:t + 2, :], v[:, t:t + 2, :]).then_inc(done, 16)
                else:
                    v = tables[ONEHOT_FEATS[ITEMS[i]] - 1].rearrange("(p t) d -> p (t d)", t=KT)
                    sp.dma_start(s[0:112, :], v[0:112, :]).then_inc(done, 16)
                    sp.dma_start(s[112:KROWS, :], v[112:KROWS, :]).then_inc(done, 16)

            def load_ids(i, n):
                t0, t1 = OH_PARTS[i]
                src = ids_onehot[t0:t1, bass.ds(n * BLOCK, BLOCK)].partition_broadcast(P)
                sp.dma_start(ids_b[:, t0:t1, :], src).then_inc(ids_ready[i], 16)

            load_idx(0, 0)
            load_idx(1, 0)
            load_ids(0, 0)
            load_item(0)
            load_item(1)
            load_ids(1, 0)
            load_dense(0, 0)
            load_dense(1, 0)
            sp.dma_start(b2_sb[:, :], b2).then_inc(small_ready, 16)
            sp.dma_start(w3[:, :], W3).then_inc(small_ready, 16)
            for i in range(2, len(ITEMS)):
                sp.wait_ge(split_low, i - 1)
                load_item(i)
            for part, (_, t1) in enumerate(OH_PARTS):
                sp.wait_ge(onehot_made, t1 * KT)
                load_ids(part, 1)
            def steps(n, ids_too):
                for j in range(2):
                    for g in range(XB):
                        gathers = len(ROW_BANKS[g]) - (g == 0)
                        sp.wait_ge(rows_ready[j][g], n * (16 * gathers) + 16 * gathers)
                    load_idx(j, n + 1)
                    sp.wait_ge(x_done, n * (2 * XB) + (XB * j + 1))
                    load_dense(j, n + 1)
                if ids_too:
                    for part, (_, t1) in enumerate(OH_PARTS):
                        sp.wait_ge(onehot_made, n * OH_ALL + (OH_ALL + t1 * KT))
                        load_ids(part, n + 2)

            with sp.Fori(0, BLOCKS - 2) as n:
                steps(n, True)
            steps(BLOCKS - 2, False)

        @block.gpsimd
        def _(pool):
            nc.gpsimd.memset(ident[:, :], 0.0).then_inc(consts_ready, 1)
            pool.wait_ge(consts_ready, 1)
            nc.gpsimd.affine_select(out=ident[:, :], in_=ident[:, :], compare_op=ALU.not_equal, fill=1.0,
                                    base=0, pattern=[[-1, P]], channel_multiplier=1).then_inc(consts_ready, 1)
            nc.gpsimd.iota(row_id[:, :], pattern=[[1, KT]], base=0, channel_multiplier=KT,
                           allow_small_or_imprecise_dtypes=True).then_inc(consts_ready, 1)

            def gather(n, first):
                for j in range(2):
                    pool.wait_ge(idx_ready[j], n * 16 + 16)
                    at = 0
                    for g, feats in enumerate(ROW_BANKS):
                        if not first:
                            pool.wait_ge(x_done, n * (2 * XB) + (XB * j + g + 1 - 2 * XB))
                            pool.sem_inc(gather_go, 1)
                        for f in feats:
                            if f:
                                nc.gpsimd.indirect_dma_start(
                                    out=rows[:, j, at, :], out_offset=None, in_=tables[f - 1],
                                    in_offset=bass.IndirectOffsetOnAxis(ap=idx[:, j, f - 1:f], axis=0),
                                ).then_inc(rows_ready[j][g], 16)
                            at += 1

            gather(0, True)
            with pool.Fori(1, BLOCKS) as n:
                gather(n, False)

        @block.tensor
        def _(pe):
            def transpose_rows(n, j):
                at = 0
                for g, feats in enumerate(ROW_BANKS):
                    gathers = len(feats) - (g == 0)
                    if g == 0:
                        pe.wait_ge(dense_ready[j], n * 16 + 16)
                    pe.wait_ge(rows_ready[j][g], n * (16 * gathers) + 16 * gathers)
                    if g == len(bank_r):
                        pe.wait_ge(x_evac_act, n * (2 * X_ACT) + (X_ACT * j + 1))
                    for i in range(len(feats)):
                        last = nc.tensor.transpose(bank_r[g % 4][:, i * SUB:(i + 1) * SUB],
                                                   rows[:, j, at, :], ident[:, :])
                        at += 1
                    last.then_inc(x_done, 1)

            def interactions(n, j, h):
                if h == 0:
                    pe.wait_ge(x_evac_act, n * (2 * X_ACT) + X_ACT * (j + 1))
                    pe.wait_ge(x_evac_dve, n * (2 * X_DVE) + X_DVE * (j + 1))
                    if j == 0:
                        pe.wait_ge(oh_evac, n * OB + OB)
                if j == 1:
                    pe.wait_ge(g_evac, n * 4 + (h + 1))
                for q in range(HALF_QUADS):
                    for s in range(COLS):
                        at = (s * 2 * HALF_QUADS + h * HALF_QUADS + q) * FEATS
                        last = nc.tensor.matmul(
                            bank_c[h][32 * s:32 * s + FEATS - 1, q * (FEATS - 1):(q + 1) * (FEATS - 1)],
                            XT[:, j, at + 1:at + FEATS], XT[:, j, at:at + FEATS - 1],
                            start=True, stop=True, tile_position=(0, 32 * s))
                last.then_inc(gram_done, 1)

            def lookup(n, t, first=False):
                g = t // 2
                if t % 2 == 0 and g >= 2:
                    pe.wait_ge(oh_evac, n * OB + (g - 1))
                if first:
                    pe.wait_ge(split_low, ITEMS.index(t) + 1)
                out = bank_oh[g % 2][:, (t % 2) * BLOCK:(t % 2 + 1) * BLOCK]
                for k in range(KT):
                    at = t * KT + k
                    if at % OH_CHUNK == 0:
                        pe.wait_ge(onehot_made, n * OH_ALL + (at + OH_CHUNK))
                    moving = onehot[0:KROWS, at % OH_RING, :]
                    nc.tensor.matmul(out, tab_high[0:KROWS, t, k, :], moving, start=(k == 0), stop=False)
                    last = nc.tensor.matmul(out, tab_low[0:KROWS, t, k, :], moving,
                                            start=False, stop=(k == KT - 1))
                    if at % OH_CHUNK == OH_CHUNK - 1:
                        last.then_inc(onehot_used, 1)

            def transpose_g(n):
                pe.wait_ge(g_evac, n * 4 + 4)
                for k, pairs in enumerate(T_PAIRS):
                    for i, c2 in enumerate(pairs):
                        both = G[:, 2 * c2:2 * c2 + 2, :].rearrange("p c q -> p (c q)")
                        last = nc.tensor.transpose(bank_t[k][:, i * P:(i + 1) * P], both, ident[:, :])
                    last.then_inc(t_done, 1)

            def transpose_z(n):
                pe.wait_ge(t_evac, n * 4 + 4)
                pe.wait_ge(pads_ready, 3)
                pe.sem_inc(z_go, 1)
                for t, (c0, size) in enumerate(Z_TILES):
                    for s in range(COLS):
                        at = (t % 2) * BLOCK + s * QUADS
                        last = nc.tensor.transpose(bank_c[t // 2][0:size, at:at + QUADS],
                                                   Z[:, s, c0:c0 + size], ident[0:QUADS, 0:QUADS])
                    if t:
                        last.then_inc(zt_done, 1)

            def split_products(out, terms):
                for i, (w_h, w_l, a_h, a_l) in enumerate(terms):
                    nc.tensor.matmul(out, w_h, a_h, start=(i == 0), stop=False)
                    nc.tensor.matmul(out, w_h, a_l, start=False, stop=False)
                    last = nc.tensor.matmul(out, w_l, a_h, start=False, stop=(i == len(terms) - 1))
                return last

            def layer1(n):
                pe.wait_ge(split_low, len(ITEMS))
                pe.wait_ge(xd_high_ready, n * 2 + 2)
                pe.wait_ge(xd_low_ready, n * 2 + 2)
                pe.wait_ge(z_high_ready, n * 2 + 2)
                pe.wait_ge(z_low_ready, n * 2 + 2)
                xh = xd_high[:, :, :].rearrange("p s q -> p (s q)")
                xl = xd_low[:, :, :].rearrange("p s q -> p (s q)")
                for m in range(HID1 // P):
                    mm = slice(m * P, (m + 1) * P)
                    terms = [(w1_high[:, 0, mm], w1_low[:, 0, mm], xh, xl)]
                    for t, (_, size) in enumerate(Z_TILES):
                        terms.append((w1_high[0:size, t + 1, mm], w1_low[0:size, t + 1, mm],
                                      zt_high[0:size, t, :], zt_low[0:size, t, :]))
                    last = split_products(bank_m[m // 2][:, (m % 2) * BLOCK:(m % 2 + 1) * BLOCK], terms)
                    if m % 2:
                        last.then_inc(l1_done, 1)

            def layer2(n):
                pe.wait_ge(h1_high_ready, n * 2 + 2)
                pe.wait_ge(h1_low_ready, n * 2 + 2)
                for m in range(HID2 // P):
                    mm = slice(m * P, (m + 1) * P)
                    terms = [(w2_high[:, t, mm], w2_low[:, t, mm], h1_high[:, t, :], h1_low[:, t, :])
                             for t in range(HID1 // P)]
                    last = split_products(bank_c[0][:, m * BLOCK:(m + 1) * BLOCK], terms)
                last.then_inc(l2_done, 1)

            def layer3(n):
                pe.wait_ge(h2_ready, n * 2 + 2)
                for m in range(HID2 // P):
                    last = nc.tensor.matmul(bank_c[1][0:1, 0:BLOCK], w3[:, m:m + 1], h2[:, m, :],
                                            start=(m == 0), stop=(m == HID2 // P - 1))
                last.then_inc(l3_done, 1)

            def steps(n, last_block):
                transpose_rows(n, 0)
                interactions(n, 0, 0)
                transpose_rows(n, 1)
                interactions(n, 0, 1)
                interactions(n, 1, 0)
                interactions(n, 1, 1)
                t = 0
                for before, stage_of in zip(OH_BEFORE, (transpose_g, transpose_z, layer1, layer2, layer3)):
                    while t < before and not last_block:
                        lookup(n + 1, t)
                        t += 1
                    stage_of(n)

            pe.wait_ge(consts_ready, 3)
            for t in range(N_OH):
                lookup(0, t, first=True)
            pe.wait_ge(small_ready, 32)
            with pe.Fori(0, BLOCKS - 1) as n:
                steps(n, False)
            steps(BLOCKS - 1, True)

        def z_copies(k):
            for i, c2 in enumerate(T_PAIRS[k]):
                for half in range(2):
                    c = 2 * c2 + half
                    src = bank_t[k][half * QUADS:(half + 1) * QUADS, i * P:(i + 1) * P]
                    src = src.rearrange("p (s f) -> p s f", s=COLS)[:, :, c:FEATS - 1]
                    yield Z[:, :, PAIR_BASE[c]:PAIR_BASE[c] + FEATS - 1 - c], src

        @block.scalar
        def _(act):
            def round_item(i):
                src, high, _ = staged(i)
                act.wait_ge(stage_in[i % 2], stage_arrived(i))
                if ITEMS[i] == W_DENSE:
                    act.wait_ge(dense_w_sum, 1)
                nc.scalar.copy(high, src).then_inc(split_high, 1)

            def lookups_to_xt(n, g):
                feats = ONEHOT_BANKS[g]
                chunks = sum(len(b) for b in ONEHOT_BANKS[:g + 1]) * KT // OH_CHUNK
                act.wait_ge(onehot_used, n * (OH_ALL // OH_CHUNK) + chunks)
                src = bank_oh[g % 2][:, 0:len(feats) * BLOCK].rearrange("p (f b) -> p f b", f=len(feats))
                for j in range(2):
                    last = nc.scalar.copy(features(xt_feat[j], feats), src[:, :, j * SUB:(j + 1) * SUB])
                last.then_inc(oh_evac, 1)

            def rows_to_xt(n, j):
                at = 0
                for g, feats in enumerate(ROW_BANKS):
                    if g in ROWS_ON_DVE:
                        continue
                    act.wait_ge(x_done, n * (2 * XB) + (XB * j + g + 1))
                    src = bank_r[g % 4][:, 0:len(feats) * SUB]
                    nc.scalar.copy(features(xt_feat[j], feats), as_pairs(src, feats)).then_inc(x_evac_act, 1)
                act.wait_ge(x_evac_act, n * (2 * X_ACT) + (X_ACT * j + 1))
                src = xt_feat[j][:, 0, :].rearrange("p (s q) -> p s q", s=COLS)
                nc.scalar.copy(xd_high[:, :, 32 * j:32 * j + 32], src).then_inc(xd_high_ready, 1)

            def t_to_z(n):
                for k in range(4):
                    act.wait_ge(t_done, n * 4 + (k + 1))
                    for dst, src in z_copies(k):
                        last = nc.scalar.copy(dst, src)
                    last.then_inc(t_evac, 1)

            def round_z(n):
                act.wait_ge(zt_done, n * 2 + 1)
                nc.scalar.copy(zt_high[:, 0:2, :],
                               bank_c[0][:, :].rearrange("p (t b) -> p t b", t=2)).then_inc(z_high_ready, 1)
                act.wait_ge(zt_done, n * 2 + 2)
                k = Z_TILES[2][1]
                nc.scalar.copy(zt_high[0:k, 2, :], bank_c[1][0:k, 0:BLOCK]).then_inc(z_high_ready, 1)

            def round_h1(n):
                for i in range(2):
                    act.wait_ge(l1_done, n * 2 + (i + 1))
                    nc.scalar.activation(h1_high[:, 2 * i:2 * i + 2, :].rearrange("p t b -> p (t b)"),
                                         bank_m[i][:, :], ACT.Relu).then_inc(h1_high_ready, 1)

            def relu_h2(n):
                act.wait_ge(l2_done, n + 1)
                for m in range(2):
                    nc.scalar.activation(h2[:, m, :], bank_c[0][:, m * BLOCK:(m + 1) * BLOCK], ACT.Relu,
                                         bias=b2_sb[:, m:m + 1]).then_inc(h2_ready, 1)

            def copy_y(n):
                act.wait_ge(l3_done, n + 1)
                src = bank_c[1][0:1, 0:BLOCK].rearrange("p (s j q) -> p j s q", s=COLS, j=2)
                dst = y_sb[:, bass.ds(n * BLOCK, BLOCK)].rearrange("p (j s q) -> p j s q", s=COLS, j=2)
                nc.scalar.copy(dst, src).then_inc(y_ready, 1)

            def steps(n, last_block):
                rows_to_xt(n, 0)
                rows_to_xt(n, 1)
                g = 0
                for before, stage_of in zip(OH_BEFORE, (t_to_z, round_z, round_h1, relu_h2, copy_y)):
                    while 2 * (g + 1) <= before and not last_block:
                        if g == 0:
                            act.wait_ge(gram_done, n * 4 + 4)
                        lookups_to_xt(n + 1, g)
                        g += 1
                    stage_of(n)

            i = 0
            for g in range(OB):
                until = ITEMS.index(min(2 * g + 3, N_OH - 1)) + 1
                for i in range(i, until):
                    round_item(i)
                i = until
                lookups_to_xt(0, g)
            act.wait_ge(small_ready, 32)
            with act.Fori(0, BLOCKS - 1) as n:
                steps(n, False)
            steps(BLOCKS - 1, True)
            act.wait_ge(y_ready, BLOCKS)
            act.dma_start(y, y_sb[:, :]).then_inc(y_out, 16)
            act.wait_ge(y_out, 16)

        @block.vector
        def _(dve):
            def remainder(i):
                src, high, low = staged(i)
                if ITEMS[i] == W_DENSE:
                    dve.wait_ge(stage_in[i % 2], stage_arrived(i))
                    s = stage[:, i % 2, :]
                    nc.vector.tensor_tensor(s[:, 0:HID1], s[:, 0:HID1], s[:, HID1:2 * HID1],
                                            ALU.add).then_inc(dense_w_sum, 1)
                dve.wait_ge(split_high, i + 1)
                nc.vector.tensor_tensor(low, src, high.bitcast(F32), ALU.subtract).then_inc(split_low, 1)

            def make_onehots(n, lo, hi, first=False):
                for at in range(lo, hi):
                    for part, (t0, _) in enumerate(OH_PARTS):
                        if at == t0 * KT:
                            dve.wait_ge(ids_ready[part], n * 16 + 16)
                    if at % OH_CHUNK == 0 and not (first and at < OH_RING):
                        dve.wait_ge(onehot_used, n * (OH_ALL // OH_CHUNK)
                                    + (at + OH_CHUNK - OH_RING) // OH_CHUNK)
                    t, k = divmod(at, KT)
                    nc.vector.tensor_scalar(onehot[0:KROWS, at % OH_RING, :], ids_b[0:KROWS, t, :],
                                            row_id[0:KROWS, k:k + 1], None,
                                            ALU.is_equal).then_inc(onehot_made, 1)

            def g_from_psum(n, j, h):
                dve.wait_ge(gram_done, n * 4 + (2 * j + h + 1))
                q0 = (2 * j + h) * HALF_QUADS
                dst = G[:, :, q0:q0 + HALF_QUADS].rearrange("p c q -> p q c")
                src = bank_c[h][:, 0:HALF_QUADS * (FEATS - 1)].rearrange("p (q c) -> p q c", q=HALF_QUADS)
                nc.vector.tensor_copy(dst, src).then_inc(g_evac, 1)

            def dense_low(n, j):
                dve.wait_ge(xd_high_ready, n * 2 + (j + 1))
                src = xt_feat[j][:, 0, :].rearrange("p (s q) -> p s q", s=COLS)
                at = slice(32 * j, 32 * j + 32)
                nc.vector.tensor_tensor(xd_low[:, :, at], src, xd_high[:, :, at].bitcast(F32),
                                        ALU.subtract).then_inc(xd_low_ready, 1)

            def rows_to_xt(n, j):
                for i, g in enumerate(ROWS_ON_DVE):
                    dve.wait_ge(x_done, n * (2 * XB) + (XB * j + g + 1))
                    feats = ROW_BANKS[g]
                    src = bank_r[g % 4][:, 0:len(feats) * SUB]
                    nc.vector.tensor_copy(features(xt_feat[j], feats),
                                          as_pairs(src, feats)).then_inc(x_evac_dve, 1)

            def z_low(n):
                dve.wait_ge(z_high_ready, n * 2 + 1)
                nc.vector.tensor_tensor(zt_low[:, 0:2, :], bank_c[0][:, :].rearrange("p (t b) -> p t b", t=2),
                                        zt_high[:, 0:2, :].bitcast(F32), ALU.subtract).then_inc(z_low_ready, 1)
                dve.wait_ge(z_high_ready, n * 2 + 2)
                k = Z_TILES[2][1]
                nc.vector.tensor_tensor(zt_low[0:k, 2, :], bank_c[1][0:k, 0:BLOCK],
                                        zt_high[0:k, 2, :].bitcast(F32), ALU.subtract).then_inc(z_low_ready, 1)

            def h1_remainder(n):
                for i in range(2):
                    dve.wait_ge(h1_high_ready, n * 2 + (i + 1))
                    high = h1_high[:, 2 * i:2 * i + 2, :].rearrange("p t b -> p (t b)")
                    low = h1_low[:, 2 * i:2 * i + 2, :].rearrange("p t b -> p (t b)")
                    nc.vector.scalar_tensor_tensor(out=low, in0=bank_m[i][:, :], scalar=0.0,
                                                   in1=high.bitcast(F32), op0=ALU.max,
                                                   op1=ALU.subtract).then_inc(h1_low_ready, 1)

            def steps(n, last_block):
                def onehots(lo, hi):
                    if not last_block:
                        make_onehots(n + 1, lo, hi)

                rows_to_xt(n, 0)
                dense_low(n, 0)
                onehots(0, 4)
                g_from_psum(n, 0, 0)
                rows_to_xt(n, 1)
                onehots(4, 8)
                g_from_psum(n, 0, 1)
                dense_low(n, 1)
                onehots(8, 12)
                g_from_psum(n, 1, 0)
                onehots(12, 16)
                g_from_psum(n, 1, 1)
                onehots(16, 34)
                z_low(n)
                onehots(34, 56)
                h1_remainder(n)
                onehots(56, OH_ALL)

            for h in range(2):
                nc.vector.memset(bank_c[h][:, :], 0.0).then_inc(pads_ready, 1)
            nc.vector.memset(Z[:, :, Z_ONE:Z_ONE + 1], 1.0).then_inc(pads_ready, 1)
            dve.wait_ge(consts_ready, 3)
            make_onehots(0, 0, KT, first=True)
            for i, what in enumerate(ITEMS):
                remainder(i)
                if what in range(1, N_OH):
                    make_onehots(0, what * KT, (what + 1) * KT, first=True)
            with dve.Fori(0, BLOCKS - 1) as n:
                steps(n, False)
            steps(BLOCKS - 1, True)


def kernel(**inputs):
    import numpy as np
    import concourse.bacc as bacc
    from concourse.bass_utils import run_bass_kernel_spmd

    nc = bacc.Bacc("TRN2", target_bir_lowering=False, num_devices=1)
    ids = np.asarray(inputs["ids"])
    arrays = {
        "dense": inputs["r_dense_features"],
        "ids": ids,
        "ids_onehot": ids.T[[f - 1 for f in ONEHOT_FEATS]],
        "W1": inputs["W_top1"],
        "b1": np.asarray(inputs["b_top1"]).reshape(1, HID1),
        "W2": inputs["W_top2"],
        "b2": np.asarray(inputs["b_top2"]).reshape(HID2 // P, P).T,
        "W3": np.asarray(inputs["W_top3"]).reshape(HID2 // P, P).T,
    }
    for t in range(N_SPARSE):
        arrays[f"tbl_{t}"] = inputs[f"tbl_{t}"]
    arrays = {k: np.ascontiguousarray(v) for k, v in arrays.items()}
    ap = {k: nc.dram_tensor(f"{k}_dram", v.shape, mybir.dt.from_np(v.dtype), kind="ExternalInput").ap()
          for k, v in arrays.items()}
    y = nc.dram_tensor("y_dram", (1, BATCH), F32, kind="ExternalOutput").ap()
    build(nc, ap["dense"], ap["ids"], ap["ids_onehot"], [ap[f"tbl_{t}"] for t in range(N_SPARSE)],
          ap["W1"], ap["b1"], ap["W2"], ap["b2"], ap["W3"], y)
    r = run_bass_kernel_spmd(nc, [{f"{k}_dram": v for k, v in arrays.items()}], core_ids=[0])
    return r.results[0]["y_dram"].reshape(BATCH, 1)
```

```python
import concourse.bass as bass
from concourse import mybir
from contextlib import ExitStack

F32 = mybir.dt.float32
F32R = mybir.dt.float32r
I32 = mybir.dt.int32
ALU = mybir.AluOpType
ACT = mybir.ActivationFunctionType

P = 128
BATCH = 2048
N_SPARSE = 26
FEATS = N_SPARSE + 1
DIM = 128
PAIRS = FEATS * (FEATS - 1) // 2
HID1, HID2 = 512, 256

SUB = 128
BLOCK = 2 * SUB
BLOCKS = BATCH // BLOCK
COLS = 4
QUADS = BLOCK // COLS
HALF_QUADS = SUB // COLS // 2

ONEHOT_BANKS = [(5, 6), (11, 13), (17, 20), (25, 26)]
ONEHOT_FEATS = [f for bank in ONEHOT_BANKS for f in bank]
N_OH = len(ONEHOT_FEATS)
OH_ROWS = 1000
KT = 8
KROWS = OH_ROWS // KT
OH_ALL = N_OH * KT
OH_RING = 16
OH_CHUNK = 4
OH_PARTS = [(0, 4), (4, N_OH)]
OH_BEFORE = (2, 4, 6, 7, N_OH)
OH_FIRST = 5
STAGES = 4
ROW_BANKS = [(0, 1, 2, 3), (4, 8, 12, 16), (7, 10, 15, 18), (9, 14, 19, 24), (21, 22, 23)]
ROWS_ON_DVE = (1, 3)
ROW_FEATS = [f for bank in ROW_BANKS for f in bank]
XB = len(ROW_BANKS)
OB = len(ONEHOT_BANKS)

Z_ONE = PAIRS
Z_COLS = PAIRS + 1
Z_TILES = [(0, 128), (128, 128), (256, Z_COLS - 256)]
PAIR_BASE = [sum(FEATS - 1 - i for i in range(c)) for c in range(FEATS)]
T_ON_ACT_LAST, T_ON_DVE_LAST = (0, 2), (1, 3)
N_PAIRED = (FEATS - 1) // 2


def features(view, feats):
    f0 = feats[0]
    steps = {b - a for a, b in zip(feats, feats[1:])}
    if len(feats) == 1:
        return view[:, f0:f0 + 1, :]
    if len(steps) == 1:
        step = steps.pop()
        return view[:, f0:feats[-1] + 1:step, :]
    inner, outer = feats[1] - f0, feats[2] - f0
    both = view[:, f0:f0 + 2 * outer, :].rearrange("p (a e) b -> p a e b", e=outer)
    return both[:, :, 0:inner + 1:inner, :]


def as_pairs(tile, feats):
    steps = {b - a for a, b in zip(feats, feats[1:])}
    if len(steps) > 1:
        return tile.rearrange("p (a e b) -> p a e b", a=2, e=2)
    return tile.rearrange("p (f b) -> p f b", f=len(feats))


def build(nc, dense, ids, ids_onehot, tables, W1, b1, W2, b2, W3, y):
    ctx = ExitStack()
    with ctx:
        def sb(name, shape, dt=F32):
            return ctx.enter_context(nc.sbuf_tensor(name, shape, dt))

        def bank(name):
            return ctx.enter_context(nc.psum_tensor(name, [P, 512], F32))

        def sem(name):
            return ctx.enter_context(nc.semaphore(name))

        ident = sb("ident", [P, P])
        row_id = sb("row_id", [P, KT])
        tab_high = sb("tab_high", [P, N_OH, KT, DIM], F32R)
        tab_low = sb("tab_low", [P, N_OH, KT, DIM], F32R)
        stage = sb("stage", [P, STAGES, KT * DIM])
        ids_b = sb("ids_b", [P, N_OH, BLOCK], I32)
        onehot = sb("onehot", [P, OH_RING, BLOCK], F32R)
        idx = sb("idx", [P, 2, N_SPARSE], I32)
        rows = sb("rows", [P, 2, len(ROW_FEATS), DIM])
        XT = sb("XT", [P, 2, SUB * FEATS])
        xd_high = sb("xd_high", [P, COLS, QUADS], F32R)
        xd_low = sb("xd_low", [P, COLS, QUADS], F32R)
        G = sb("G", [P, FEATS - 1, QUADS])
        Z = sb("Z", [QUADS, COLS, Z_COLS])
        zt_high = sb("zt_high", [P, 3, BLOCK], F32R)
        zt_low = sb("zt_low", [P, 3, BLOCK], F32R)
        w1_high = sb("w1_high", [P, 4, HID1], F32R)
        w1_low = sb("w1_low", [P, 4, HID1], F32R)
        w2_high = sb("w2_high", [P, 4, HID2], F32R)
        w2_low = sb("w2_low", [P, 4, HID2], F32R)
        w3 = sb("w3", [P, 2])
        b2_sb = sb("b2_sb", [P, 2])
        h1_high = sb("h1_high", [P, 4, BLOCK], F32R)
        h1_low = sb("h1_low", [P, 4, BLOCK], F32R)
        h2 = sb("h2", [P, 2, BLOCK])
        assert STAGES * KT * DIM >= BATCH
        y_sb = stage[0:1, :, :].rearrange("p i n -> p (i n)")[:, 0:BATCH]

        bank_x = [bank(f"bank_x{i}") for i in range(2)]
        bank_oh = [bank(f"bank_oh{i}") for i in range(2)]
        bank_c = [bank(f"bank_c{i}") for i in range(2)]
        bank_m = [bank(f"bank_m{i}") for i in range(2)]
        bank_t = [bank_c[0], bank_c[1], bank_m[0], bank_m[1]]
        bank_r = [bank_x[0], bank_x[1], bank_m[0], bank_m[1]]
        T_PAIRS = [range(4 * k, min(4 * k + 4, N_PAIRED)) for k in range(4)]

        consts_ready = sem("consts_ready")
        pads_ready = sem("pads_ready")
        small_ready = sem("small_ready")
        stage_in = [sem(f"stage_in{i}") for i in range(STAGES)]
        dense_w_sum = sem("dense_w_sum")
        split_high = sem("split_high")
        split_low = sem("split_low")
        idx_ready = [sem(f"idx_ready{j}") for j in range(2)]
        dense_ready = [sem(f"dense_ready{j}") for j in range(2)]
        rows_ready = [[sem(f"rows_ready{j}_{g}") for g in range(XB)] for j in range(2)]
        gather_go = sem("gather_go")
        ids_ready = [sem(f"ids_ready{i}") for i in range(2)]
        onehot_made = sem("onehot_made")
        onehot_used = sem("onehot_used")
        oh_evac = sem("oh_evac")
        x_done = sem("x_done")
        x_evac_act = sem("x_evac_act")
        x_evac_dve = sem("x_evac_dve")
        X_ACT, X_DVE = XB - len(ROWS_ON_DVE), len(ROWS_ON_DVE)
        xd_high_ready = sem("xd_high_ready")
        xd_low_ready = sem("xd_low_ready")
        gram_done = sem("gram_done")
        g_evac = sem("g_evac")
        t_done = sem("t_done")
        t_evac = sem("t_evac")
        zt_done = sem("zt_done")
        z_go = sem("z_go")
        z_high_ready = sem("z_high_ready")
        z_low_ready = sem("z_low_ready")
        l1_done = sem("l1_done")
        h1_high_ready = sem("h1_high_ready")
        h1_low_ready = sem("h1_low_ready")
        l2_done = sem("l2_done")
        h2_ready = sem("h2_ready")
        l3_done = sem("l3_done")
        c1_free = sem("c1_free")
        y_out = sem("y_out")

        W_DENSE, W_PAIRS_A, W_PAIRS_B, W_2 = "dense", "pairs_a", "pairs_b", "w2"
        ITEMS = list(range(N_OH)) + [W_DENSE, W_PAIRS_A, W_PAIRS_B, W_2]

        def staged(i):
            s, what = stage[:, i % STAGES, :], ITEMS[i]
            if what == W_DENSE:
                return s[:, 0:HID1], w1_high[:, 0, :], w1_low[:, 0, :]
            if what == W_PAIRS_A:
                v = s.rearrange("p (t n) -> p t n", t=2)
                return v, w1_high[:, 1:3, :], w1_low[:, 1:3, :]
            if what == W_PAIRS_B:
                k = Z_TILES[2][1]
                return s[0:k, 0:HID1], w1_high[0:k, 3, :], w1_low[0:k, 3, :]
            if what == W_2:
                return s.rearrange("p (t n) -> p t n", t=4), w2_high[:, :, :], w2_low[:, :, :]
            v = s.rearrange("p (t d) -> p t d", t=KT)
            return v[0:KROWS], tab_high[0:KROWS, what], tab_low[0:KROWS, what]

        def stage_arrived(i):
            return 32 * (i // STAGES + 1)

        xt_feat = [XT[:, j, :].rearrange("p (b f) -> p f b", f=FEATS) for j in range(2)]

        block = ctx.enter_context(nc.Block())

        @block.sync
        def _(sp):
            def load_idx(j, n):
                at = n * BLOCK + j * SUB
                sp.dma_start(idx[:, j, :], ids[bass.ds(at, SUB), :]).then_inc(idx_ready[j], 16)

            def load_dense(j, n):
                at = n * BLOCK + j * SUB
                sp.dma_start(rows[:, j, 0, :], dense[bass.ds(at, SUB), :]).then_inc(dense_ready[j], 16)

            def load_item(i):
                s = stage[:, i % STAGES, :]
                done = stage_in[i % STAGES]
                if ITEMS[i] == W_DENSE:
                    sp.dma_start(s[:, 0:HID1], W1[0:DIM, :]).then_inc(done, 16)
                    sp.dma_start(s[:, HID1:2 * HID1], W1[DIM + PAIRS:, :]).then_inc(done, 16)
                elif ITEMS[i] == W_PAIRS_A:
                    for t in range(2):
                        sp.dma_start(s[:, t * HID1:(t + 1) * HID1],
                                     W1[DIM + t * P:DIM + (t + 1) * P, :]).then_inc(done, 16)
                elif ITEMS[i] == W_PAIRS_B:
                    k = Z_TILES[2][1] - 1
                    sp.dma_start(s[0:k, 0:HID1], W1[DIM + 2 * P:DIM + PAIRS, :]).then_inc(done, 16)
                    sp.dma_start(s[k:k + 1, 0:HID1], b1).then_inc(done, 16)
                elif ITEMS[i] == W_2:
                    v = W2.rearrange("(t p) n -> p t n", p=P)
                    sv = s.rearrange("p (t n) -> p t n", t=4)
                    for t in range(0, 4, 2):
                        sp.dma_start(sv[:, t:t + 2, :], v[:, t:t + 2, :]).then_inc(done, 16)
                else:
                    v = tables[ONEHOT_FEATS[ITEMS[i]] - 1].rearrange("(p t) d -> p (t d)", t=KT)
                    sp.dma_start(s[0:112, :], v[0:112, :]).then_inc(done, 16)
                    sp.dma_start(s[112:KROWS, :], v[112:KROWS, :]).then_inc(done, 16)

            def load_ids(i, n):
                t0, t1 = OH_PARTS[i]
                src = ids_onehot[t0:t1, bass.ds(n * BLOCK, BLOCK)].partition_broadcast(P)
                sp.dma_start(ids_b[:, t0:t1, :], src).then_inc(ids_ready[i], 16)

            load_idx(0, 0)
            load_idx(1, 0)
            load_ids(0, 0)
            for i in range(STAGES):
                load_item(i)
                if i == 1:
                    load_ids(1, 0)
            load_dense(0, 0)
            load_dense(1, 0)
            sp.dma_start(b2_sb[:, :], b2).then_inc(small_ready, 16)
            sp.dma_start(w3[:, :], W3).then_inc(small_ready, 16)
            for i in range(STAGES, len(ITEMS)):
                sp.wait_ge(split_low, i - STAGES + 1)
                load_item(i)
            for part, (_, t1) in enumerate(OH_PARTS):
                sp.wait_ge(onehot_made, t1 * KT)
                load_ids(part, 1)

            def steps(n, ids_too):
                for j in range(2):
                    for g in range(XB):
                        gathers = len(ROW_BANKS[g]) - (g == 0)
                        sp.wait_ge(rows_ready[j][g], n * (16 * gathers) + 16 * gathers)
                    load_idx(j, n + 1)
                    sp.wait_ge(x_done, n * (2 * XB) + (XB * j + 1))
                    load_dense(j, n + 1)
                if ids_too:
                    for part, (_, t1) in enumerate(OH_PARTS):
                        sp.wait_ge(onehot_made, n * OH_ALL + (OH_ALL + t1 * KT))
                        load_ids(part, n + 2)

            with sp.Fori(0, BLOCKS - 2) as n:
                steps(n, True)
            steps(BLOCKS - 2, False)

        @block.gpsimd
        def _(pool):
            nc.gpsimd.memset(ident[:, :], 0.0).then_inc(consts_ready, 1)
            pool.wait_ge(consts_ready, 1)
            nc.gpsimd.affine_select(out=ident[:, :], in_=ident[:, :], compare_op=ALU.not_equal, fill=1.0,
                                    base=0, pattern=[[-1, P]], channel_multiplier=1).then_inc(consts_ready, 1)
            nc.gpsimd.iota(row_id[:, :], pattern=[[1, KT]], base=0, channel_multiplier=KT,
                           allow_small_or_imprecise_dtypes=True).then_inc(consts_ready, 1)

            def gather(n, first):
                for j in range(2):
                    pool.wait_ge(idx_ready[j], n * 16 + 16)
                    at = 0
                    for g, feats in enumerate(ROW_BANKS):
                        if not first:
                            pool.wait_ge(x_done, n * (2 * XB) + (XB * j + g + 1 - 2 * XB))
                            pool.sem_inc(gather_go, 1)
                        for f in feats:
                            if f:
                                nc.gpsimd.indirect_dma_start(
                                    out=rows[:, j, at, :], out_offset=None, in_=tables[f - 1],
                                    in_offset=bass.IndirectOffsetOnAxis(ap=idx[:, j, f - 1:f], axis=0),
                                ).then_inc(rows_ready[j][g], 16)
                            at += 1

            gather(0, True)
            with pool.Fori(1, BLOCKS) as n:
                gather(n, False)

        @block.tensor
        def _(pe):
            def transpose_rows(n, j):
                at = 0
                for g, feats in enumerate(ROW_BANKS):
                    gathers = len(feats) - (g == 0)
                    if g == 0:
                        pe.wait_ge(dense_ready[j], n * 16 + 16)
                    pe.wait_ge(rows_ready[j][g], n * (16 * gathers) + 16 * gathers)
                    if g == len(bank_r):
                        pe.wait_ge(x_evac_act, n * (2 * X_ACT) + (X_ACT * j + 1))
                    for i in range(len(feats)):
                        last = nc.tensor.transpose(bank_r[g % 4][:, i * SUB:(i + 1) * SUB],
                                                   rows[:, j, at, :], ident[:, :])
                        at += 1
                    last.then_inc(x_done, 1)

            def interactions(n, j, h):
                if h == 0:
                    pe.wait_ge(x_evac_act, n * (2 * X_ACT) + X_ACT * (j + 1))
                    pe.wait_ge(x_evac_dve, n * (2 * X_DVE) + X_DVE * (j + 1))
                    if j == 0:
                        pe.wait_ge(oh_evac, n * OB + OB)
                if j == 0 and h == 1:
                    pe.wait_ge(c1_free, n + 1)
                if j == 1:
                    pe.wait_ge(g_evac, n * 4 + (h + 1))
                for q in range(HALF_QUADS):
                    for s in range(COLS):
                        at = (s * 2 * HALF_QUADS + h * HALF_QUADS + q) * FEATS
                        last = nc.tensor.matmul(
                            bank_c[h][32 * s:32 * s + FEATS - 1, q * (FEATS - 1):(q + 1) * (FEATS - 1)],
                            XT[:, j, at + 1:at + FEATS], XT[:, j, at:at + FEATS - 1],
                            start=True, stop=True, tile_position=(0, 32 * s))
                last.then_inc(gram_done, 1)

            def lookup(n, t, first=False):
                g = t // 2
                if t % 2 == 0 and g >= 2:
                    pe.wait_ge(oh_evac, n * OB + (g - 1))
                if first:
                    pe.wait_ge(split_low, ITEMS.index(t) + 1)
                out = bank_oh[g % 2][:, (t % 2) * BLOCK:(t % 2 + 1) * BLOCK]
                for k in range(KT):
                    at = t * KT + k
                    if at % OH_CHUNK == 0:
                        pe.wait_ge(onehot_made, n * OH_ALL + (at + OH_CHUNK))
                    moving = onehot[0:KROWS, at % OH_RING, :]
                    nc.tensor.matmul(out, tab_high[0:KROWS, t, k, :], moving, start=(k == 0), stop=False)
                    last = nc.tensor.matmul(out, tab_low[0:KROWS, t, k, :], moving,
                                            start=False, stop=(k == KT - 1))
                    if at % OH_CHUNK == OH_CHUNK - 1:
                        last.then_inc(onehot_used, 1)

            def transpose_g(n):
                pe.wait_ge(g_evac, n * 4 + 4)
                for k, pairs in enumerate(T_PAIRS):
                    for i, c2 in enumerate(pairs):
                        both = G[:, 2 * c2:2 * c2 + 2, :].rearrange("p c q -> p (c q)")
                        last = nc.tensor.transpose(bank_t[k][:, i * P:(i + 1) * P], both, ident[:, :])
                    last.then_inc(t_done, 1)

            def transpose_z(n):
                pe.wait_ge(t_evac, n * 4 + 4)
                pe.sem_inc(z_go, 1)
                for t, (c0, size) in enumerate(Z_TILES):
                    for s in range(COLS):
                        at = (t % 2) * BLOCK + s * QUADS
                        last = nc.tensor.transpose(bank_c[t // 2][0:size, at:at + QUADS],
                                                   Z[:, s, c0:c0 + size], ident[0:QUADS, 0:QUADS])
                    if t:
                        last.then_inc(zt_done, 1)

            def split_product(out, w_h, w_l, a_h, a_l, first, last, low_ready=None):
                nc.tensor.matmul(out, w_h, a_h, start=first, stop=False)
                nc.tensor.matmul(out, w_l, a_h, start=False, stop=False)
                if low_ready:
                    pe.wait_ge(*low_ready)
                return nc.tensor.matmul(out, w_h, a_l, start=False, stop=last)

            def layer1(n):
                pe.wait_ge(split_low, len(ITEMS))
                pe.wait_ge(xd_high_ready, n * 2 + 2)
                pe.wait_ge(xd_low_ready, n * 2 + 2)
                xh = xd_high[:, :, :].rearrange("p s q -> p (s q)")
                xl = xd_low[:, :, :].rearrange("p s q -> p (s q)")
                for m in range(HID1 // P):
                    mm = slice(m * P, (m + 1) * P)
                    out = bank_m[m // 2][:, (m % 2) * BLOCK:(m % 2 + 1) * BLOCK]
                    split_product(out, w1_high[:, 0, mm], w1_low[:, 0, mm], xh, xl, True, False)
                    for t, (_, size) in enumerate(Z_TILES):
                        low_ready = None
                        if m == 0 and t != 1:
                            pe.wait_ge(z_high_ready, n * 2 + (1 + t // 2))
                            low_ready = (z_low_ready, n * 2 + (1 + t // 2))
                        last = split_product(out, w1_high[0:size, t + 1, mm], w1_low[0:size, t + 1, mm],
                                             zt_high[0:size, t, :], zt_low[0:size, t, :],
                                             False, t == len(Z_TILES) - 1, low_ready)
                    if m % 2:
                        last.then_inc(l1_done, 1)

            def layer2(n):
                for m in range(HID2 // P):
                    mm = slice(m * P, (m + 1) * P)
                    out = bank_c[0][:, m * BLOCK:(m + 1) * BLOCK]
                    for t in range(HID1 // P):
                        low_ready = None
                        if m == 0 and t % 2 == 0:
                            pe.wait_ge(h1_high_ready, n * 2 + (1 + t // 2))
                            low_ready = (h1_low_ready, n * 2 + (1 + t // 2))
                        last = split_product(out, w2_high[:, t, mm], w2_low[:, t, mm],
                                             h1_high[:, t, :], h1_low[:, t, :],
                                             t == 0, t == HID1 // P - 1, low_ready)
                last.then_inc(l2_done, 1)

            def layer3(n):
                for m in range(HID2 // P):
                    pe.wait_ge(h2_ready, n * 2 + (m + 1))
                    last = nc.tensor.matmul(bank_c[1][0:1, 0:BLOCK], w3[:, m:m + 1], h2[:, m, :],
                                            start=(m == 0), stop=(m == HID2 // P - 1))
                last.then_inc(l3_done, 1)

            def steps(n, last_block):
                interactions(n, 0, 0)
                interactions(n, 0, 1)
                transpose_rows(n, 1)
                if not last_block:
                    lookup(n + 1, 0)
                interactions(n, 1, 0)
                interactions(n, 1, 1)
                t = 1
                for before, stage_of in zip(OH_BEFORE, (transpose_g, transpose_z, layer1, layer2, layer3)):
                    if stage_of == layer3 and not last_block:
                        transpose_rows(n + 1, 0)
                    while t < before and not last_block:
                        lookup(n + 1, t)
                        t += 1
                    stage_of(n)

            pe.wait_ge(consts_ready, 3)
            for t in range(N_OH):
                if t == OH_FIRST:
                    transpose_rows(0, 0)
                lookup(0, t, first=True)
            pe.wait_ge(pads_ready, 2)
            pe.wait_ge(small_ready, 32)
            with pe.Fori(0, BLOCKS - 1) as n:
                steps(n, False)
            steps(BLOCKS - 1, True)

        def z_copies(k):
            for i, c2 in enumerate(T_PAIRS[k]):
                for half in range(2):
                    c = 2 * c2 + half
                    src = bank_t[k][half * QUADS:(half + 1) * QUADS, i * P:(i + 1) * P]
                    src = src.rearrange("p (s f) -> p s f", s=COLS)[:, :, c:FEATS - 1]
                    yield Z[:, :, PAIR_BASE[c]:PAIR_BASE[c] + FEATS - 1 - c], src

        @block.scalar
        def _(act):
            def round_item(i):
                src, high, _ = staged(i)
                act.wait_ge(stage_in[i % STAGES], stage_arrived(i))
                if ITEMS[i] == W_DENSE:
                    act.wait_ge(dense_w_sum, 1)
                nc.scalar.copy(high, src).then_inc(split_high, 1)

            def lookups_to_xt(n, g):
                feats = ONEHOT_BANKS[g]
                chunks = sum(len(b) for b in ONEHOT_BANKS[:g + 1]) * KT // OH_CHUNK
                act.wait_ge(onehot_used, n * (OH_ALL // OH_CHUNK) + chunks)
                src = bank_oh[g % 2][:, 0:len(feats) * BLOCK].rearrange("p (f b) -> p f b", f=len(feats))
                for j in range(2):
                    last = nc.scalar.copy(features(xt_feat[j], feats), src[:, :, j * SUB:(j + 1) * SUB])
                last.then_inc(oh_evac, 1)

            def rows_to_xt(n, j):
                at = 0
                for g, feats in enumerate(ROW_BANKS):
                    if g in ROWS_ON_DVE:
                        continue
                    act.wait_ge(x_done, n * (2 * XB) + (XB * j + g + 1))
                    src = bank_r[g % 4][:, 0:len(feats) * SUB]
                    nc.scalar.copy(features(xt_feat[j], feats), as_pairs(src, feats)).then_inc(x_evac_act, 1)
                act.wait_ge(x_evac_act, n * (2 * X_ACT) + (X_ACT * j + 1))
                src = xt_feat[j][:, 0, :].rearrange("p (s q) -> p s q", s=COLS)
                nc.scalar.copy(xd_high[:, :, 32 * j:32 * j + 32], src).then_inc(xd_high_ready, 1)

            def t_to_z(n, banks):
                for k in banks:
                    act.wait_ge(t_done, n * 4 + (k + 1))
                    for dst, src in z_copies(k):
                        last = nc.scalar.copy(dst, src)
                    last.then_inc(t_evac, 1)

            def round_z(n):
                act.wait_ge(zt_done, n * 2 + 1)
                nc.scalar.copy(zt_high[:, 0:2, :],
                               bank_c[0][:, :].rearrange("p (t b) -> p t b", t=2)).then_inc(z_high_ready, 1)
                act.wait_ge(zt_done, n * 2 + 2)
                k = Z_TILES[2][1]
                nc.scalar.copy(zt_high[0:k, 2, :], bank_c[1][0:k, 0:BLOCK]).then_inc(z_high_ready, 1)

            def round_h1(n):
                for i in range(2):
                    act.wait_ge(l1_done, n * 2 + (i + 1))
                    nc.scalar.activation(h1_high[:, 2 * i:2 * i + 2, :].rearrange("p t b -> p (t b)"),
                                         bank_m[i][:, :], ACT.Relu).then_inc(h1_high_ready, 1)

            def relu_h2(n):
                act.wait_ge(l2_done, n + 1)
                for m in range(2):
                    nc.scalar.activation(h2[:, m, :], bank_c[0][:, m * BLOCK:(m + 1) * BLOCK], ACT.Relu,
                                         bias=b2_sb[:, m:m + 1]).then_inc(h2_ready, 1)

            def copy_y(n):
                act.wait_ge(l3_done, n + 1)
                src = bank_c[1][0:1, 0:BLOCK].rearrange("p (s j q) -> p j s q", s=COLS, j=2)
                dst = y_sb[:, bass.ds(n * BLOCK, BLOCK)].rearrange("p (j s q) -> p j s q", s=COLS, j=2)
                nc.scalar.copy(dst, src).then_inc(c1_free, 1)

            def steps(n, last_block):
                rows_to_xt(n, 1)
                g = 0
                for before, stage_of in zip(OH_BEFORE, (t_to_z, round_z, round_h1, relu_h2, copy_y)):
                    if stage_of == copy_y and not last_block:
                        rows_to_xt(n + 1, 0)
                    while 2 * (g + 1) <= before and not last_block:
                        if g == 0:
                            act.wait_ge(gram_done, n * 4 + 4)
                        lookups_to_xt(n + 1, g)
                        g += 1
                    if stage_of == t_to_z:
                        t_to_z(n, T_ON_ACT_LAST if last_block else range(4))
                    else:
                        stage_of(n)

            lookups_after = {min(2 * g + 3, N_OH): g for g in range(OB)}
            for i in range(len(ITEMS)):
                round_item(i)
                if i == OH_FIRST + 1:
                    rows_to_xt(0, 0)
                if i in lookups_after:
                    lookups_to_xt(0, lookups_after[i])
            act.wait_ge(small_ready, 32)
            with act.Fori(0, BLOCKS - 1) as n:
                steps(n, False)
            steps(BLOCKS - 1, True)
            act.wait_ge(c1_free, BLOCKS + 1)
            act.dma_start(y, y_sb[:, :]).then_inc(y_out, 16)
            act.wait_ge(y_out, 16)

        @block.vector
        def _(dve):
            def remainder(i):
                src, high, low = staged(i)
                if ITEMS[i] == W_DENSE:
                    dve.wait_ge(stage_in[i % STAGES], stage_arrived(i))
                    s = stage[:, i % STAGES, :]
                    nc.vector.tensor_tensor(s[:, 0:HID1], s[:, 0:HID1], s[:, HID1:2 * HID1],
                                            ALU.add).then_inc(dense_w_sum, 1)
                dve.wait_ge(split_high, i + 1)
                nc.vector.tensor_tensor(low, src, high.bitcast(F32), ALU.subtract).then_inc(split_low, 1)

            def make_onehots(n, lo, hi, first=False):
                for at in range(lo, hi):
                    for part, (t0, _) in enumerate(OH_PARTS):
                        if at == t0 * KT:
                            dve.wait_ge(ids_ready[part], n * 16 + 16)
                    if at % OH_CHUNK == 0 and not (first and at < OH_RING):
                        dve.wait_ge(onehot_used, n * (OH_ALL // OH_CHUNK)
                                    + (at + OH_CHUNK - OH_RING) // OH_CHUNK)
                    t, k = divmod(at, KT)
                    nc.vector.tensor_scalar(onehot[0:KROWS, at % OH_RING, :], ids_b[0:KROWS, t, :],
                                            row_id[0:KROWS, k:k + 1], None,
                                            ALU.is_equal).then_inc(onehot_made, 1)

            def g_from_psum(n, j, h):
                dve.wait_ge(gram_done, n * 4 + (2 * j + h + 1))
                q0 = (2 * j + h) * HALF_QUADS
                dst = G[:, :, q0:q0 + HALF_QUADS].rearrange("p c q -> p q c")
                src = bank_c[h][:, 0:HALF_QUADS * (FEATS - 1)].rearrange("p (q c) -> p q c", q=HALF_QUADS)
                nc.vector.tensor_copy(dst, src).then_inc(g_evac, 1)

            def dense_low(n, j):
                dve.wait_ge(xd_high_ready, n * 2 + (j + 1))
                src = xt_feat[j][:, 0, :].rearrange("p (s q) -> p s q", s=COLS)
                at = slice(32 * j, 32 * j + 32)
                nc.vector.tensor_tensor(xd_low[:, :, at], src, xd_high[:, :, at].bitcast(F32),
                                        ALU.subtract).then_inc(xd_low_ready, 1)

            def rows_to_xt(n, j):
                for i, g in enumerate(ROWS_ON_DVE):
                    dve.wait_ge(x_done, n * (2 * XB) + (XB * j + g + 1))
                    feats = ROW_BANKS[g]
                    src = bank_r[g % 4][:, 0:len(feats) * SUB]
                    nc.vector.tensor_copy(features(xt_feat[j], feats),
                                          as_pairs(src, feats)).then_inc(x_evac_dve, 1)

            def t_to_z(n, banks):
                for k in banks:
                    dve.wait_ge(t_done, n * 4 + (k + 1))
                    for dst, src in z_copies(k):
                        last = nc.vector.tensor_copy(dst, src)
                    last.then_inc(t_evac, 1)

            def z_low(n):
                dve.wait_ge(z_high_ready, n * 2 + 1)
                nc.vector.tensor_tensor(zt_low[:, 0:2, :], bank_c[0][:, :].rearrange("p (t b) -> p t b", t=2),
                                        zt_high[:, 0:2, :].bitcast(F32), ALU.subtract).then_inc(z_low_ready, 1)
                dve.wait_ge(z_high_ready, n * 2 + 2)
                k = Z_TILES[2][1]
                nc.vector.tensor_tensor(zt_low[0:k, 2, :], bank_c[1][0:k, 0:BLOCK],
                                        zt_high[0:k, 2, :].bitcast(F32), ALU.subtract).then_inc(z_low_ready, 1)

            def h1_remainder(n):
                for i in range(2):
                    dve.wait_ge(h1_high_ready, n * 2 + (i + 1))
                    high = h1_high[:, 2 * i:2 * i + 2, :].rearrange("p t b -> p (t b)")
                    low = h1_low[:, 2 * i:2 * i + 2, :].rearrange("p t b -> p (t b)")
                    nc.vector.scalar_tensor_tensor(out=low, in0=bank_m[i][:, :], scalar=0.0,
                                                   in1=high.bitcast(F32), op0=ALU.max,
                                                   op1=ALU.subtract).then_inc(h1_low_ready, 1)

            def steps(n, last_block):
                def onehots(lo, hi):
                    if not last_block:
                        make_onehots(n + 1, lo, hi)

                onehots(0, 4)
                g_from_psum(n, 0, 0)
                onehots(4, 8)
                g_from_psum(n, 0, 1)
                rows_to_xt(n, 1)
                dense_low(n, 1)
                onehots(8, 12)
                g_from_psum(n, 1, 0)
                onehots(12, 16)
                g_from_psum(n, 1, 1)
                onehots(16, 46)
                if last_block:
                    t_to_z(n, T_ON_DVE_LAST)
                z_low(n)
                onehots(46, 56)
                h1_remainder(n)
                onehots(56, OH_ALL)
                if not last_block:
                    rows_to_xt(n + 1, 0)
                    dense_low(n + 1, 0)

            nc.vector.memset(bank_c[0][:, :], 0.0).then_inc(pads_ready, 1)
            nc.vector.memset(bank_c[1][:, :], 0.0).then_inc(c1_free, 1)
            nc.vector.memset(Z[:, :, Z_ONE:Z_ONE + 1], 1.0).then_inc(pads_ready, 1)
            dve.wait_ge(consts_ready, 3)
            make_onehots(0, 0, 2 * KT, first=True)
            for i, what in enumerate(ITEMS):
                remainder(i)
                if what in range(2, N_OH):
                    make_onehots(0, what * KT, (what + 1) * KT, first=True)
                if what == OH_FIRST:
                    rows_to_xt(0, 0)
                    dense_low(0, 0)
            with dve.Fori(0, BLOCKS - 1) as n:
                steps(n, False)
            steps(BLOCKS - 1, True)


def kernel(**inputs):
    import numpy as np
    import concourse.bacc as bacc
    from concourse.bass_utils import run_bass_kernel_spmd

    nc = bacc.Bacc("TRN2", target_bir_lowering=False, num_devices=1)
    ids = np.asarray(inputs["ids"])
    arrays = {
        "dense": inputs["r_dense_features"],
        "ids": ids,
        "ids_onehot": ids.T[[f - 1 for f in ONEHOT_FEATS]],
        "W1": inputs["W_top1"],
        "b1": np.asarray(inputs["b_top1"]).reshape(1, HID1),
        "W2": inputs["W_top2"],
        "b2": np.asarray(inputs["b_top2"]).reshape(HID2 // P, P).T,
        "W3": np.asarray(inputs["W_top3"]).reshape(HID2 // P, P).T,
    }
    for t in range(N_SPARSE):
        arrays[f"tbl_{t}"] = inputs[f"tbl_{t}"]
    arrays = {k: np.ascontiguousarray(v) for k, v in arrays.items()}
    ap = {k: nc.dram_tensor(f"{k}_dram", v.shape, mybir.dt.from_np(v.dtype), kind="ExternalInput").ap()
          for k, v in arrays.items()}
    y = nc.dram_tensor("y_dram", (1, BATCH), F32, kind="ExternalOutput").ap()
    build(nc, ap["dense"], ap["ids"], ap["ids_onehot"], [ap[f"tbl_{t}"] for t in range(N_SPARSE)],
          ap["W1"], ap["b1"], ap["W2"], ap["b2"], ap["W3"], y)
    r = run_bass_kernel_spmd(nc, [{f"{k}_dram": v for k, v in arrays.items()}], core_ids=[0])
    return r.results[0]["y_dram"].reshape(BATCH, 1)
```
